# Optimizing a Trainium2 kernel written in Bass

```python
import numpy as np
import jax
import jax.numpy as jnp

def _softmax(x, axis=-1):
    return jax.nn.softmax(x, axis=axis)
def _gelu(x):
    return jax.nn.gelu(x, approximate=True)
def _silu(x):
    return jax.nn.silu(x)
def _sigmoid(x):
    return jax.nn.sigmoid(x)
def _layernorm(x, axis=-1, eps=1e-5):
    m = jnp.mean(x, axis=axis, keepdims=True)
    v = jnp.var(x, axis=axis, keepdims=True)
    return (x - m) / jnp.sqrt(v + eps)
def _scatter_add(tgt, idx, src, axis=0):
    return tgt.at[idx].add(src)
def _segment_sum(src, seg, n):
    return jax.ops.segment_sum(src, seg, n)

kernel_name = 'mk_adj_resnorm_d1_adj_256_c655f7'

def setup_inputs(seed: int = 0):
    np.random.seed(seed)
    _w = jnp.asarray
    def _rec_inputs():
        import jax
        import jax.numpy as jnp
        _gk = jax.random.key(seed)
        x = -0.0005207 + 1.001 * jax.random.normal(jax.random.fold_in(_gk, 1), (8, 2048, 256), jnp.float32)
        _a = jax.random.bernoulli(jax.random.fold_in(_gk, 2), 0.015625, (8, 2048, 2048))
        _a = jnp.logical_or(_a, jnp.swapaxes(_a, -1, -2))
        _a = jnp.logical_or(_a, jnp.eye(2048, dtype=bool))
        adj = _a.astype(jnp.int32)
        return x, adj
    x, adj = _rec_inputs()
    def _L0_gnn_setup():
        import jax, jax.numpy as jnp
        import numpy as np
        NEG_INF = -1000000000.0
        LRELU_ALPHA = 0.2
        key = jax.random.key(seed)
        k1, k2, k3, k4, k5 = jax.random.split(key, 5)
        B, N, Din, H, F = (8, 1024, 256, 4, 64)
        X = jax.random.normal(k1, (B, N, Din), dtype=jnp.float32)
        A = jax.random.randint(k2, (B, N, N), 0, 2).astype(jnp.int32)
        W = jax.random.normal(k3, (Din, H * F), dtype=jnp.float32) * np.sqrt(2.0 / (Din + H * F))
        a_src = jax.random.normal(k4, (H, F), dtype=jnp.float32) * np.sqrt(2.0 / (1 + F))
        a_dst = jax.random.normal(k5, (H, F), dtype=jnp.float32) * np.sqrt(2.0 / (1 + F))
        return {'X': X, 'A': A, 'W': W, 'a_src': a_src, 'a_dst': a_dst}
    _L0_gnn_all = _L0_gnn_setup()
    _L0_gnn_in = {k: v for k, v in _L0_gnn_all.items() if k in ('W', 'a_src', 'a_dst', )}
    del _L0_gnn_all

    return {
        "x": x,
        "adj": adj,
        "L0_gnn_W": _L0_gnn_in["W"],
        "L0_gnn_a_src": _L0_gnn_in["a_src"],
        "L0_gnn_a_dst": _L0_gnn_in["a_dst"],
    }

def reference(x, adj, L0_gnn_W, L0_gnn_a_src, L0_gnn_a_dst):
    import jax
    import jax.numpy as jnp
    def _L0_gnn_ref(X, A, W, a_src, a_dst):
        import jax, jax.numpy as jnp
        import numpy as np
        NEG_INF = -1000000000.0
        LRELU_ALPHA = 0.2
        B, N, _ = X.shape
        H, F = a_src.shape
        Wh = (X @ W).reshape(B, N, H, F)
        e_src = jnp.einsum('bnhf,hf->bnh', Wh, a_src)
        e_dst = jnp.einsum('bjhf,hf->bjh', Wh, a_dst)
        e = jax.nn.leaky_relu(e_src[:, :, None, :] + e_dst[:, None, :, :], LRELU_ALPHA)
        mask = (A > 0)[..., None]
        e = jnp.where(mask, e, NEG_INF)
        alpha = jax.nn.softmax(e, axis=2)
        Hout = jnp.einsum('bijh,bjhf->bihf', alpha, Wh)
        Hout = jax.nn.elu(Hout)
        return Hout.reshape(B, N, H * F)

    x = _layernorm(x + _L0_gnn_ref(x, adj, L0_gnn_W, L0_gnn_a_src, L0_gnn_a_dst), axis=-1)
    return x


_drawn_inputs = setup_inputs


def setup_inputs(seed=0):
    import zlib

    import numpy as np

    out = dict(_drawn_inputs(seed))
    spreads = {}
    factors = {}
    for name, (base, spread) in spreads.items():
        noise = np.random.default_rng([zlib.crc32(name.encode()), seed]).standard_normal(out[name].shape)
        drawn = base * np.exp(spread * noise) if base else spread * noise
        out[name] = jnp.asarray(drawn.astype(out[name].dtype))
    for name, factor in factors.items():
        out[name] = (out[name] * factor).astype(out[name].dtype)
    return out
```

```python
import numpy as np
import concourse.bass as bass
from concourse import mybir
from contextlib import ExitStack

F32, F16, BF16 = mybir.dt.float32, mybir.dt.float16, mybir.dt.bfloat16
F8, I32, U8 = mybir.dt.float8e4, mybir.dt.int32, mybir.dt.uint8
ALU, ACT, AX = mybir.AluOpType, mybir.ActivationFunctionType, mybir.AxisListType

ON_SCALAR = (4, 3, 3, 3)


def gat_resnorm(nc, x, adj, w, a_src, a_dst, out):
    B, N, D = x.shape
    H, F = a_src.shape
    P = 128
    NK = N // (2 * P)
    NJ = 2 * NK
    HALF = N // 2
    NI = HALF // P
    C = F + 1
    UB = 2 * H
    NCH = NK // 2
    NP = NI // 2
    DC = D // P
    WC = D + 2 * H
    SLOPE = 0.2
    ONE = 8
    BIG = float(2.0 ** 100)
    VSCALE = float(2.0 ** 14)
    TINY = float(2.0 ** -80)
    ONES = ONE * 0x01010101

    x_pairs = x.rearrange("b (k p e) d -> b k p e d", p=P, e=2)
    out_pairs = out.rearrange("b (k p e) d -> b k p e d", p=P, e=2)
    adj_tiles = adj.rearrange("b (t p) j -> (b t) p j", p=P)
    s_rows = nc.dram_tensor("s_rows", (B, H, N), F32).ap()

    ctx = ExitStack()
    with ctx:
        def sb(name, shape, dt):
            return ctx.enter_context(nc.sbuf_tensor(name, shape, dt))

        def pb(name, shape, dt):
            return ctx.enter_context(nc.psum_tensor(name, shape, dt))

        def sem(name):
            return ctx.enter_context(nc.semaphore(name))

        pos = sb("pos", [P, 2, NK, 2 * HALF], U8)
        neg = sb("neg", [P, 2, NK, 2 * HALF], U8)
        sign = sb("sign", [P, 2, 2, 2 * HALF], U8)
        adjT = sb("adjT", [P, 2, NK, 2 * HALF], U8)
        adj_in = sb("adj_in", [P, 2, N], BF16)
        adj_code = sb("adj_code", [P, 2, N], U8)
        values = sb("values", [P, H, NJ, 2, 2 * C], F16)
        wh = sb("wh", [P, NJ, H, C], F32)
        sd = sb("sd", [P, 2 * H, NK, 2], F32)
        s_bc = sb("s_bc", [P, 2, HALF], F32)
        x_in = sb("x_in", [P, 2, 2, D], F32)
        xT = sb("xT", [P, 2, DC, P], F32)
        w_aug = sb("w_aug", [P, DC, WC], F32)
        sums = sb("sums", [P, 2, 2, 2, 2 * C], F32)
        part = sb("part", [P, 2, 2, C], F32)
        row = sb("row", [P, NI, C], F32)
        heads = sb("heads", [P, 2, NI, H * F], F32)
        resid = sb("resid", [P, 2, 2, D], F32)
        expo = sb("expo", [P, 2, D], F32)
        scaled = sb("scaled", [P, NK, C], F32)
        wh_sum = sb("wh_sum", [P, 2, H, F], F32)
        mean_w = sb("mean_w", [P, P], F32)
        id32 = sb("id32", [P, P], F32)
        id16 = sb("id16", [P, P], BF16)
        ones = sb("ones", [P, NJ * H], F32)
        neg_d = sb("neg_d", [P, H, NK, 2], F32)
        big_d = sb("big_d", [P, H, NK, 2], F32)
        shifted = sb("shifted", [P, H, NJ], F32)
        above = sb("above", [P, 3, H, NJ], F32)
        edge = sb("edge", [P, 2, H, NJ], F32)
        edge_n = sb("edge_n", [P, 2, H, NJ], F32)
        alpha_next = sb("alpha_next", [P, 2, H, NJ], F32)
        alpha = sb("alpha", [P, 2, H, NJ], F32)
        fold_next = sb("fold_next", [P, H, C], F32)
        fold = sb("fold", [P, H, C], F32)
        small = sb("small", [P, 64], F32)
        top, top_all = small[:, 0:H + 1], small[:, 5:5 + H + 1]
        w_top = small[:, 10:14]
        recip, recip_w = small[:, 14:14 + NI], small[:, 22:22 + NI]
        stats = small[:, 30:42].rearrange("p (t n) -> p t n", t=2)
        moments = small[:, 42:46].rearrange("p (t n) -> p t n", t=2)
        var_eps, rstd, minus_half = small[:, 46:48], small[:, 48:50], small[:, 50:52]
        sT = wh_sum[0:H * NK, 0, :, :].rearrange("p h f -> p (h f)").rearrange("p (n e) -> p n e", e=2)
        a_bc = values[:, 0, :, :, :].rearrange("p a b c -> p (a b c)").bitcast(F32)[:, 0:2 * H * F]
        a_prod = values[:, 1, :, :, :].rearrange("p a b c -> p (a b c)").bitcast(F32)[:, 0:H * F]

        acc = pb("acc", [P, 4, 512], F32)
        adj_ps = pb("adj_ps", [P, 2, NK, P], BF16)
        wh_ps = pb("wh_ps", [P, 512], F32)
        x_ps = pb("x_ps", [P, 512], F32)
        xT_ps = x_ps[:, 0:DC * P].rearrange("p (c n) -> p c n", c=DC)
        sT_ps = x_ps[0:H * NK, DC * P:DC * P + 2 * P].rearrange("p (e n) -> p e n", e=2)

        waits_passed = sem("waits_passed")
        w_loaded = sem("w_loaded")
        x_loaded = [sem(f"x_loaded{i}") for i in range(2)]
        s_loaded = [sem(f"s_loaded{i}") for i in range(2)]
        resid_loaded = [sem(f"resid_loaded{i}") for i in range(2)]
        adj_loaded = [sem(f"adj_loaded{i}") for i in range(2)]
        s_stored = sem("s_stored")
        out_stored = [sem(f"out_stored{i}") for i in range(2)]
        consts_made = sem("consts_made")
        waug_made = sem("waug_made")
        adj_coded = sem("adj_coded")
        adj_turned = sem("adj_turned")
        adj_kept = sem("adj_kept")
        x_turned = sem("x_turned")
        x_kept = sem("x_kept")
        wh_made = sem("wh_made")
        wh_kept = sem("wh_kept")
        s_turned = sem("s_turned")
        s_kept = sem("s_kept")
        d_flipped = sem("d_flipped")
        big_made = sem("big_made")
        scalar_signs = sem("scalar_signs")
        vector_signs = sem("vector_signs")
        masks_made = sem("masks_made")
        sums_made = sem("sums_made")
        sums_kept = sem("sums_kept")
        sums_read = sem("sums_read")
        part_steps = sem("part_steps")
        recip_made = sem("recip_made")
        heads_made = sem("heads_made")
        value_steps = sem("value_steps")
        values_made = sem("values_made")
        tops_made = sem("tops_made")
        tops_shared = sem("tops_shared")
        factor_steps = sem("factor_steps")
        exps_made = sem("exps_made")
        wh_added = sem("wh_added")
        mean_made = sem("mean_made")
        fold_made = sem("fold_made")
        latched = sem("latched")
        wtop_latched = sem("wtop_latched")
        resid_less = sem("resid_less")
        elu_exp = sem("elu_exp")
        norm_steps = sem("norm_steps")
        rstd_made = sem("rstd_made")
        out_made = sem("out_made")

        NCONST = 9
        NF = 9
        NS = 7
        NADD = NJ // 2 - 1

        def due(count):
            return not isinstance(count, int) or count > 0

        def apart(eng):
            eng.sem_inc(waits_passed, 1)

        def batches(eng, body):
            body(0, True, False)
            with eng.Fori(1, B - 1) as b:
                body(b, False, False)
            body(B - 1, False, True)

        X_TILES = {3: range(0, 6), 4: range(6, 12), 5: range(12, NJ)}

        block = ctx.enter_context(nc.Block())

        @block.sync
        def _(sp):
            def load_x(b, q):
                if due(NJ * b + 2 * (q - 1)):
                    sp.wait_ge(x_turned, NJ * b + 2 * (q - 1))
                apart(sp)
                sp.dma_start(x_in[:, q % 2, :, :], x_pairs[b, q, :, :, :]).then_inc(x_loaded[q % 2], 16)

            def load_s(b, k):
                u = UB * b + k
                if k == 0:
                    sp.wait_ge(s_stored, 16 * (b + 1))
                if due(NCH * (u - 1)):
                    sp.wait_ge(scalar_signs, NCH * (u - 1))
                apart(sp)
                if due((4 * NCH - sum(ON_SCALAR)) * (u - 1)):
                    sp.wait_ge(vector_signs, (4 * NCH - sum(ON_SCALAR)) * (u - 1))
                apart(sp)
                half, h = k // H, k % H
                sp.dma_start(s_bc[:, k % 2, :],
                             s_rows[b, h:h + 1, half * HALF:(half + 1) * HALF].to_broadcast([P, HALF])
                             ).then_inc(s_loaded[k % 2], 16)

            def store_s(b):
                sp.wait_ge(s_kept, b + 1)
                apart(sp)
                sp.dma_start(s_rows[b, :, :].rearrange("h (k n) -> (h k) n", k=NK),
                             wh_sum[0:H * NK, 0, :, :].rearrange("p h f -> p (h f)")).then_inc(s_stored, 16)

            def load_resid(b, k):
                if due(8 * (UB * b + k - k % 2)):
                    sp.wait_ge(out_stored[k % 2], 8 * (UB * b + k - k % 2))
                apart(sp)
                sp.dma_start(resid[:, k % 2, :, :], x_pairs[b, k, :, :, :]).then_inc(resid_loaded[k % 2], 16)

            def store_out(b, k):
                r = UB * b + k
                sp.wait_ge(out_made, 2 * (r + 1))
                apart(sp)
                sp.dma_start(out_pairs[b, k, :, :, :], resid[:, k % 2, :, :]).then_inc(out_stored[k % 2], 16)

            for c in range(DC):
                sp.dma_start(w_aug[:, c, 0:D], w[c * P:(c + 1) * P, :]).then_inc(w_loaded, 16)
            for i, a in enumerate((a_src, a_dst)):
                sp.dma_start(a_bc[:, i * H * F:(i + 1) * H * F],
                             a.rearrange("(o h) f -> o (h f)", o=1).to_broadcast([P, H * F])
                             ).then_inc(w_loaded, 16)
            for q in range(NK):
                load_x(0, q)
            store_s(0)
            load_s(0, 0)
            load_s(0, 1)

            def slot(b, k, first, last):
                if k < UB - 2:
                    load_s(b, k + 2)
                elif not last:
                    if k == UB - 2:
                        store_s(b + 1)
                    load_s(b + 1, k + 2 - UB)
                if not (first and k < 5):
                    store_out(b if k >= 5 else b - 1, (k - 5) % UB)
                if not (first and k < 3):
                    load_resid(b if k >= 3 else b - 1, (k - 3) % UB)
                if not last:
                    for q in {2: (0, 1), 3: (2, 3, 4), 4: (5, 6, 7)}.get(k, ()):
                        load_x(b + 1, q)

            def body(b, first, last):
                for k in range(UB):
                    slot(b, k, first, last)

            batches(sp, body)
            for k in range(3, UB):
                store_out(B - 1, k)
                if k + 2 < UB and k >= 3:
                    load_resid(B - 1, k + 2)
            for i in range(2):
                sp.wait_ge(out_stored[i], 16 * UB * B // 2)

        @block.gpsimd
        def _(pool):
            def load_adj(n, i):
                if due(n - 1):
                    pool.wait_ge(adj_coded, n - 1)
                pool.dma_start(adj_in[:, i, :], adj_tiles[n, :, :]).then_inc(adj_loaded[i], 16)

            def value_step(b, h, i, after):
                g, t0 = i // 2, (i % 2) * NK
                step = 4 * (H * b + h) + i
                if i == 0:
                    pool.wait_ge(factor_steps, NF * (b + 1))
                    if after is not None:
                        if due(NP * after):
                            pool.wait_ge(sums_made, NP * after)
                hi = values[:, h, t0:t0 + NK, g, 0:C]
                lo = values[:, h, t0:t0 + NK, g, C:2 * C]
                if due(step):
                    pool.wait_ge(values_made, step)
                pool.tensor_tensor(scaled[:, :, :], wh[:, t0:t0 + NK, h, :],
                                   edge_n[:, g, h, t0:t0 + NK].unsqueeze(2).to_broadcast([P, NK, C]),
                                   ALU.mult).then_inc(value_steps, 1)
                pool.wait_ge(value_steps, 2 * step + 1)
                apart(pool)
                pool.tensor_scalar(hi, scaled[:, :, :], 1.0, 0.0, ALU.mult, ALU.add).then_inc(value_steps, 1)
                pool.wait_ge(value_steps, 2 * step + 2)
                pool.tensor_tensor(lo, scaled[:, :, :], hi, ALU.subtract).then_inc(values_made, 1)

            def share_tops(b):
                pool.wait_ge(tops_made, 2 * (b + 1))
                apart(pool)
                pool.partition_all_reduce(top_all[:, :], top[:, :], P, bass.bass_isa.ReduceOp.max
                                          ).then_inc(tops_shared, 1)

            def add_wh(b):
                pool.wait_ge(wh_kept, 2 * NJ * (b + 1))
                pool.wait_ge(s_stored, 16 * (b + 1))
                for i in range(NADD):
                    a = wh[:, 0:2, :, 0:F] if i == 0 else wh_sum[:, :, :, :]
                    if due(NADD * b + i):
                        pool.wait_ge(wh_added, NADD * b + i)
                    pool.tensor_tensor(wh_sum[:, :, :, :], a, wh[:, 2 * i + 2:2 * i + 4, :, 0:F],
                                       ALU.add).then_inc(wh_added, 1)

            def latch(b):
                if due(UB * b):
                    pool.wait_ge(heads_made, UB * b)
                pool.wait_ge(exps_made, 4 * (b + 1))
                pool.wait_ge(fold_made, b + 1)
                if due(3 * NP * UB * b):
                    pool.wait_ge(part_steps, 3 * NP * UB * b)
                apart(pool)
                pool.tensor_scalar(alpha[:, :, :, :], alpha_next[:, :, :, :], 1.0, 0.0, ALU.mult, ALU.add
                                   ).then_inc(latched, 1)
                pool.tensor_scalar(fold[:, :, :], fold_next[:, :, :], 1.0, 0.0, ALU.mult, ALU.add
                                   ).then_inc(latched, 1)
                pool.wait_ge(latched, 2 * (b + 1))

            def epilogue(b, k, c):
                half, h, i = k // H, k % H, c % 2
                m = NP * (UB * b + k) + c
                t0 = half * NI + 2 * c
                s = sums[:, i, :, :, :]
                pool.wait_ge(sums_kept, m + 1)
                if due(3 * m):
                    pool.wait_ge(part_steps, 3 * m)
                pool.tensor_tensor(part[:, :, :, :], s[:, :, :, 0:C], s[:, :, :, C:2 * C], ALU.add
                                   ).then_inc(sums_read, 1)
                pool.wait_ge(sums_read, m + 1)
                al = alpha[:, :, h, t0:t0 + 2].rearrange("p g t -> p t g").unsqueeze(3)
                pool.tensor_tensor(part[:, :, :, :], part[:, :, :, :], al.to_broadcast([P, 2, 2, C]),
                                   ALU.mult).then_inc(part_steps, 1)
                pool.wait_ge(part_steps, 3 * m + 1)
                r = row[:, 2 * c:2 * c + 2, :]
                pool.tensor_tensor(r, part[:, :, 0, :], part[:, :, 1, :], ALU.add).then_inc(part_steps, 1)
                pool.wait_ge(part_steps, 3 * m + 2)
                pool.tensor_tensor(r, r, fold[:, h, :].unsqueeze(1).to_broadcast([P, 2, C]), ALU.add
                                   ).then_inc(part_steps, 1)

            def finish_heads(b, k):
                half, h = k // H, k % H
                u = UB * b + k
                pool.wait_ge(recip_made, 2 * (u + 1))
                if due(2 * (UB * b + half * H - H)):
                    pool.wait_ge(out_made, 2 * (UB * b + half * H - H))
                pool.tensor_tensor(heads[:, half, :, h * F:(h + 1) * F], row[:, :, 0:F],
                                   recip_w[:, :].unsqueeze(2).to_broadcast([P, NI, F]), ALU.mult
                                   ).then_inc(heads_made, 1)
                pool.wait_ge(heads_made, u + 1)

            def less_one(b, k):
                pool.wait_ge(resid_loaded[k % 2], 8 * (UB * b + k - k % 2) + 16)
                apart(pool)
                pool.tensor_scalar(resid[:, k % 2, :, :], resid[:, k % 2, :, :], 1.0, -1.0, ALU.mult, ALU.add
                                   ).then_inc(resid_less, 1)

            def inv_std(b, k):
                r = UB * b + k
                pool.wait_ge(norm_steps, NS * (r + 1))
                pool.tensor_tensor(rstd[:, :], var_eps[:, :], minus_half[:, :], ALU.pow).then_inc(rstd_made, 1)

            for ident in (id32, id16):
                pool.memset(ident[:, :], 0.0).then_inc(consts_made, 1)
            pool.memset(mean_w[:, :], TINY / N).then_inc(consts_made, 1)
            pool.memset(minus_half[:, :], -0.5).then_inc(consts_made, 1)
            pool.memset(ones[:, :], 1.0).then_inc(consts_made, 1)
            pool.memset(fold_next[:, :, :], TINY).then_inc(consts_made, 1)
            pool.memset(wh[:, :, :, F:C], 1.0).then_inc(consts_made, 1)
            pool.wait_ge(consts_made, NCONST - 2)
            for ident in (id32, id16):
                pool.affine_select(out=ident[:, :], in_=ident[:, :], compare_op=ALU.not_equal, fill=1.0, base=0,
                                   pattern=[[-1, P]], channel_multiplier=1).then_inc(consts_made, 1)
            for n in range(NI + 4):
                load_adj(n, n % 2)
            share_tops(0)
            add_wh(0)
            for i in range(4):
                value_step(0, 0, i, None)

            def slot(b, k, first, last):
                if not (first and k == 0):
                    finish_heads(b if k else b - 1, (k - 1) % UB)
                if k == 0:
                    latch(b)
                if not (first and k < 4):
                    less_one(b if k >= 4 else b - 1, (k - 4) % UB)
                for c in range(NP):
                    epilogue(b, k, c)
                    if k < H - 1:
                        value_step(b, k + 1, c, UB * b - H + k + 2)
                    if k == UB - 1 and not last:
                        value_step(b + 1, 0, c, UB * b + H + 1)
                    if c < 2 and (not last or k < H - 2):
                        load_adj(2 * NI * b + 2 * k + NI + 4 + c, c)
                    if c == 1 and k == UB - 2 and not last:
                        share_tops(b + 1)
                        add_wh(b + 1)
                if not (first and k < 4):
                    inv_std(b if k >= 4 else b - 1, (k - 4) % UB)

            def body(b, first, last):
                for k in range(UB):
                    slot(b, k, first, last)

            batches(pool, body)
            finish_heads(B - 1, UB - 1)
            for k in range(4, UB):
                less_one(B - 1, k)
                inv_std(B - 1, k)

        @block.scalar
        def _(act):
            def keep_xT(b, j):
                act.wait_ge(x_turned, NJ * b + j + 1)
                if due(NJ * b + j - 1):
                    act.wait_ge(wh_made, NJ * b + j - 1)
                act.activation(xT[:, j % 2, :, :], xT_ps, ACT.Copy).then_inc(x_kept, 1)

            def keep_wh(b, j):
                act.wait_ge(wh_made, NJ * b + j + 1)
                if j == 0:
                    if due(4 * H * b):
                        act.wait_ge(values_made, 4 * H * b)
                    if due(NADD * b):
                        act.wait_ge(wh_added, NADD * b)
                    if due(NF * b):
                        act.wait_ge(factor_steps, NF * b)
                    if due(b):
                        act.wait_ge(d_flipped, b)
                    if due(b):
                        act.wait_ge(s_turned, b)
                act.activation(wh[:, j, :, 0:F], wh_ps[:, 0:D].rearrange("p (h f) -> p h f", h=H), ACT.Copy
                               ).then_inc(wh_kept, 1)
                act.activation(sd[:, :, j // 2, j % 2], wh_ps[:, D:WC], ACT.Copy).then_inc(wh_kept, 1)

            def factor_exps(b):
                def f(n):
                    act.wait_ge(factor_steps, NF * b + n)
                if due(2 * b):
                    act.wait_ge(latched, 2 * b)
                f(4)
                act.activation(edge[:, 0, :, :], shifted[:, :, :], ACT.Exp).then_inc(exps_made, 1)
                act.activation(edge[:, 1, :, :], shifted[:, :, :], ACT.Exp, scale=SLOPE).then_inc(exps_made, 1)
                f(7)
                act.activation(alpha_next[:, 0, :, :], above[:, 1, :, :], ACT.Exp, scale=1 - SLOPE
                               ).then_inc(exps_made, 1)
                act.activation(alpha_next[:, 1, :, :], above[:, 2, :, :], ACT.Exp, scale=SLOPE - 1
                               ).then_inc(exps_made, 1)

            def make_big(b):
                act.wait_ge(wh_kept, 2 * NJ * (b + 1))
                if due(NCH * UB * b):
                    act.wait_ge(scalar_signs, NCH * UB * b)
                act.activation(big_d[:, :, :, :], sd[:, H:2 * H, :, :], ACT.Copy, scale=BIG).then_inc(big_made, 1)
                act.wait_ge(big_made, b + 1)

            def signs(b, k, c):
                h = k % H
                m = NCH * (UB * b + k) + c
                if c == 0:
                    act.wait_ge(s_loaded[k % 2], 8 * (UB * b + k - k % 2) + 16)
                if due(2 * (m - 1)):
                    act.wait_ge(masks_made, 2 * (m - 1))
                apart(act)
                for i in range(ON_SCALAR[c]):
                    kk, e = i // 2, i % 2
                    a = act.activation(sign[:, c % 2, kk, e:2 * HALF:2].bitcast(F8), s_bc[:, k % 2, :], ACT.Relu,
                                       bias=big_d[:, h, 2 * c + kk, e:e + 1], scale=BIG, saturate=False)
                a.then_inc(scalar_signs, 1)

            def keep_sums(b, k, c):
                m = NP * (UB * b + k) + c
                bank = (2 * c) % 4
                act.wait_ge(sums_made, m + 1)
                if due(m - 1):
                    act.wait_ge(sums_read, m - 1)
                act.activation(sums[:, c % 2, :, :, :].rearrange("p t g n -> p t (g n)"),
                               acc[:, bank:bank + 2, 0:4 * C], ACT.Copy).then_inc(sums_kept, 1)

            def elu_part(b, k):
                half, c, r = k // H, k % H, UB * b + k
                act.wait_ge(heads_made, UB * b + (half + 1) * H)
                if due(NS * (r - 1) + 2):
                    act.wait_ge(norm_steps, NS * (r - 1) + 2)
                act.activation(expo[:, :, :], heads[:, half, 2 * c:2 * c + 2, :], ACT.Exp).then_inc(elu_exp, 1)

            for j in range(NJ):
                keep_xT(0, j)
                keep_wh(0, j)
            make_big(0)
            factor_exps(0)
            for c in range(NCH):
                signs(0, 0, c)

            def slot(b, k, first, last):
                more = not (last and k == UB - 1)
                nb, nk = (b, k + 1) if k < UB - 1 else (b + 1, 0)
                tiles = list(X_TILES.get(k, ())) if not last else []
                if k == UB - 1 and more:
                    make_big(nb)
                for c in range(NCH):
                    for j in tiles[2 * c:2 * c + 2]:
                        keep_xT(b + 1, j)
                        keep_wh(b + 1, j)
                    if more:
                        signs(nb, nk, c)
                    keep_sums(b, k, c)
                    if c == 3 and k == UB - 2 and not last:
                        factor_exps(b + 1)
                    if c == 2 and not (first and k < 4):
                        elu_part(b if k >= 4 else b - 1, (k - 4) % UB)

            def body(b, first, last):
                for k in range(UB):
                    slot(b, k, first, last)

            batches(act, body)
            for k in range(4, UB):
                elu_part(B - 1, k)

        @block.vector
        def _(dve):
            def code_adj(n, i):
                dve.wait_ge(adj_loaded[i], 8 * (n - i) + 16)
                if due(n - 1):
                    dve.wait_ge(adj_turned, n - 1)
                dve.tensor_scalar(adj_code[:, i, :], adj_in[:, i, :], 0.0, float(ONE - 1),
                                  ALU.is_gt, ALU.add).then_inc(adj_coded, 1)

            def keep_adj(n, i, g, half, t):
                dve.wait_ge(adj_turned, n + 1)
                if due(2 * NCH * H * (g - 1)):
                    dve.wait_ge(masks_made, 2 * NCH * H * (g - 1))
                dve.tensor_copy(adjT[:, half, :, 2 * t * P:2 * (t + 1) * P].bitcast(I32),
                                adj_ps[:, i, :, :].bitcast(I32)).then_inc(adj_kept, 1)

            def keep_s(b):
                dve.wait_ge(s_turned, b + 1)
                if due(b):
                    dve.wait_ge(mean_made, b)
                dve.tensor_copy(sT.rearrange("p n e -> p e n"), sT_ps).then_inc(s_kept, 1)

            def tops(b):
                dve.wait_ge(wh_kept, 2 * NJ * (b + 1))
                if due(b):
                    dve.wait_ge(tops_shared, b)
                dve.tensor_reduce(top[:, 0:H], sd[:, H:2 * H, :, :], AX.XY, ALU.max).then_inc(tops_made, 1)
                dve.tensor_reduce(top[:, H:H + 1], wh[:, :, :, 0:F], AX.XYZ, ALU.max,
                                  apply_absolute_value=True).then_inc(tops_made, 1)

            def factors(b):
                n = [0]

                def step(ins):
                    n[0] += 1
                    ins.then_inc(factor_steps, 1)
                    dve.wait_ge(factor_steps, NF * b + n[0])

                s = sd[:, 0:H, :, :].rearrange("p h k e -> p h (k e)")
                d = sd[:, H:2 * H, :, :].rearrange("p h k e -> p h (k e)")
                D_bc = top_all[:, 0:H].unsqueeze(2).to_broadcast([P, H, NJ])
                dve.wait_ge(tops_shared, b + 1)
                if due(b):
                    dve.wait_ge(wtop_latched, b)
                step(dve.tensor_scalar(w_top[:, 0:1], top_all[:, H:H + 1], 1e-30, None, ALU.max))
                step(dve.reciprocal(w_top[:, 1:2], w_top[:, 0:1]))
                step(dve.tensor_scalar(w_top[:, 2:3], w_top[:, 1:2], VSCALE, None, ALU.mult))
                step(dve.tensor_tensor(shifted[:, :, :], d, D_bc, ALU.subtract))
                step(dve.tensor_tensor(above[:, 0, :, :], s, D_bc, ALU.add))
                step(dve.tensor_scalar(above[:, 1, :, :], above[:, 0, :, :], 0.0, None, ALU.min))
                step(dve.tensor_scalar(above[:, 2, :, :], above[:, 0, :, :], 0.0, None, ALU.max))

            def factors_end(b):
                dve.tensor_scalar(wh[:, :, :, F], ones[:, :].rearrange("p (j h) -> p j h", h=H), w_top[:, 0:1], None,
                                  ALU.mult).then_inc(factor_steps, 1)
                dve.wait_ge(exps_made, 4 * b + 2)
                if due(4 * H * b):
                    dve.wait_ge(values_made, 4 * H * b)
                dve.tensor_scalar(edge_n[:, :, :, :], edge[:, :, :, :], w_top[:, 2:3], None, ALU.mult
                                  ).then_inc(factor_steps, 1)

            def make_fold(b):
                dve.wait_ge(mean_made, b + 1)
                if due(2 * b):
                    dve.wait_ge(latched, 2 * b)
                dve.tensor_scalar(fold_next[:, :, 0:F], wh_ps[:, 0:H * F].rearrange("p (h f) -> p h f", h=H),
                                  w_top[:, 1:2], None, ALU.mult).then_inc(fold_made, 1)

            def flip_d(b):
                if due((4 * NCH - sum(ON_SCALAR)) * UB * b):
                    dve.wait_ge(vector_signs, (4 * NCH - sum(ON_SCALAR)) * UB * b)
                dve.tensor_scalar(neg_d[:, :, :, :], sd[:, H:2 * H, :, :], -1.0, None, ALU.mult
                                  ).then_inc(d_flipped, 1)
                dve.wait_ge(d_flipped, b + 1)

            def signs(b, k, c):
                h = k % H
                m = NCH * (UB * b + k) + c
                if c == 0:
                    dve.wait_ge(s_loaded[k % 2], 8 * (UB * b + k - k % 2) + 16)
                for i in range(ON_SCALAR[c], 4):
                    kk, e = i // 2, i % 2
                    if due(2 * (m - 1)):
                        dve.wait_ge(masks_made, 2 * (m - 1))
                    dve.tensor_scalar(sign[:, c % 2, kk, e:2 * HALF:2], s_bc[:, k % 2, :],
                                      neg_d[:, h, 2 * c + kk, e:e + 1], float(ONE), ALU.is_gt, ALU.mult
                                      ).then_inc(vector_signs, 1)

            def masks(b, k, c):
                half, u = k // H, UB * b + k
                m = NCH * u + c
                per_unit = 4 * NCH - sum(ON_SCALAR)
                if c == 0:
                    dve.wait_ge(adj_kept, NI * (2 * b + half + 1))
                    if due(NP * (u - 1)):
                        dve.wait_ge(sums_made, NP * (u - 1))
                dve.wait_ge(scalar_signs, m + 1)
                if due(per_unit * u + sum(4 - n for n in ON_SCALAR[0:c + 1])):
                    dve.wait_ge(vector_signs, per_unit * u + sum(4 - n for n in ON_SCALAR[0:c + 1]))

                def words(t):
                    return t.rearrange("p k n -> p (k n)").bitcast(I32)
                sg = words(sign[:, c % 2, :, :])
                ad = words(adjT[:, half, 2 * c:2 * c + 2, :])
                dve.tensor_tensor(words(pos[:, k % 2, 2 * c:2 * c + 2, :]), sg, ad, ALU.bitwise_and
                                  ).then_inc(masks_made, 1)
                dve.scalar_tensor_tensor(words(neg[:, k % 2, 2 * c:2 * c + 2, :]), sg, ONES, ad,
                                         ALU.bitwise_xor, ALU.bitwise_and).then_inc(masks_made, 1)

            def make_recip(b, k):
                u = UB * b + k
                dve.wait_ge(part_steps, 3 * NP * (u + 1))
                if due(u):
                    dve.wait_ge(heads_made, u)
                dve.reciprocal(recip[:, :], row[:, :, F]).then_inc(recip_made, 1)
                dve.wait_ge(recip_made, 2 * u + 1)
                dve.tensor_scalar(recip_w[:, :], recip[:, :], w_top[:, 3:4], None, ALU.mult).then_inc(recip_made, 1)

            def latch_top(b):
                dve.wait_ge(factor_steps, NF * b + 1)
                if due(2 * UB * b):
                    dve.wait_ge(recip_made, 2 * UB * b)
                dve.tensor_copy(w_top[:, 3:4], w_top[:, 0:1]).then_inc(wtop_latched, 1)
                dve.wait_ge(wtop_latched, b + 1)

            def norm_start(b, k):
                half, c, i, r = k // H, k % H, k % 2, UB * b + k
                n = [0]

                def step(ins):
                    n[0] += 1
                    ins.then_inc(norm_steps, 1)

                dve.wait_ge(elu_exp, r + 1)
                dve.wait_ge(resid_less, r + 1)
                res = resid[:, i, :, :]
                step(dve.scalar_tensor_tensor(expo[:, :, :], expo[:, :, :], 1.0, res, ALU.min, ALU.add))
                dve.wait_ge(norm_steps, NS * r + 1)
                step(dve.scalar_tensor_tensor(res, heads[:, half, 2 * c:2 * c + 2, :], 0.0, expo[:, :, :],
                                              ALU.max, ALU.add))
                dve.wait_ge(norm_steps, NS * r + 2)
                for t in range(2):
                    step(dve.bn_stats(stats[:, t, :], resid[:, i, t, :]))
                dve.wait_ge(norm_steps, NS * r + 4)
                apart(dve)
                for t in range(2):
                    step(dve.bn_aggr(moments[:, t, :], stats[:, t, :]))
                dve.wait_ge(norm_steps, NS * r + 6)
                if due(r):
                    dve.wait_ge(rstd_made, r)
                step(dve.tensor_scalar(var_eps[:, :], moments[:, :, 1], 1e-5, None, ALU.add))

            def norm_end(b, k):
                i, r = k % 2, UB * b + k
                dve.wait_ge(rstd_made, r + 1)
                for t in range(2):
                    dve.tensor_scalar(resid[:, i, t, :], resid[:, i, t, :], moments[:, t, 0:1], rstd[:, t:t + 1],
                                      ALU.subtract, ALU.mult).then_inc(out_made, 1)
                dve.wait_ge(out_made, 2 * (r + 1))

            dve.wait_ge(w_loaded, 16 * (DC + 2))
            done = 0
            for c in range(DC):
                for i in range(2):
                    if due(done):
                        dve.wait_ge(waug_made, done)
                    dve.tensor_tensor(a_prod, w_aug[:, c, 0:D], a_bc[:, i * D:(i + 1) * D], ALU.mult
                                      ).then_inc(waug_made, 1)
                    dve.wait_ge(waug_made, done + 1)
                    dve.tensor_reduce(w_aug[:, c, D + i * H:D + (i + 1) * H],
                                      a_prod.rearrange("p (h f) -> p h f", h=H), AX.X, ALU.add
                                      ).then_inc(waug_made, 1)
                    done += 2
            for n in range(NI):
                code_adj(n, n % 2)
                if n:
                    keep_adj(n - 1, (n - 1) % 2, 0, 0, n - 1)
            keep_adj(NI - 1, (NI - 1) % 2, 0, 0, NI - 1)
            for n in range(NI, NI + 2):
                code_adj(n, n % 2)
            keep_s(0)
            tops(0)
            flip_d(0)
            factors(0)
            factors_end(0)
            make_fold(0)
            for c in range(NCH):
                signs(0, 0, c)
                masks(0, 0, c)
            for n in range(NI, NI + 2):
                keep_adj(n, n % 2, 1, 1, n - NI)
                code_adj(n + 2, n % 2)

            def slot(b, k, first, last):
                more = not (last and k == UB - 1)
                nb, nk = (b, k + 1) if k < UB - 1 else (b + 1, 0)
                turn = not last or k < H - 1
                code = not last or k < H - 2
                n0 = 2 * NI * b + 2 * k + NI + 2
                g = 2 * nb + nk // H + 1
                half, t0 = (nk // H + 1) % 2, 2 * (nk % H)
                if k == UB - 1 and more:
                    flip_d(nb)
                for c in range(NCH):
                    if more:
                        signs(nb, nk, c)
                        masks(nb, nk, c)
                    if c == 0 and not (first and k == 0):
                        make_recip(b if k else b - 1, (k - 1) % UB)
                    if c == 0 and k == 0:
                        latch_top(b)
                    if c == 0 and not (first and k < 5):
                        norm_end(b if k >= 5 else b - 1, (k - 5) % UB)
                    if c == 1 and turn:
                        keep_adj(n0, 0, g, half, t0)
                    if c == 3 and not (first and k < 4):
                        norm_start(b if k >= 4 else b - 1, (k - 4) % UB)
                    if c == 3 and turn:
                        keep_adj(n0 + 1, 1, g, half, t0 + 1)
                    if c in (2, 3) and code:
                        code_adj(n0 + c, c % 2)
                    if k == UB - 2 and not last:
                        if c == 0:
                            keep_s(b + 1)
                            tops(b + 1)
                        if c == 2:
                            factors(b + 1)
                    if k == UB - 1 and not last and c == 0:
                        factors_end(b + 1)
                    if k == UB - 1 and not last and c == 2:
                        make_fold(b + 1)

            def body(b, first, last):
                for k in range(UB):
                    slot(b, k, first, last)

            batches(dve, body)
            make_recip(B - 1, UB - 1)
            norm_end(B - 1, 3)
            for k in range(4, UB):
                norm_start(B - 1, k)
                norm_end(B - 1, k)

        @block.tensor
        def _(pe):
            def turn_adj(n, i):
                pe.wait_ge(adj_coded, n + 1)
                if due(n - 1):
                    pe.wait_ge(adj_kept, n - 1)
                for kk in range(NK):
                    t = pe.transpose(adj_ps[:, i, kk, :],
                                     adj_code[:, i, 2 * P * kk:2 * P * (kk + 1)].bitcast(BF16), id16[:, :])
                t.then_inc(adj_turned, 1)

            def turn_x(b, j):
                q = j // 2
                if j % 2 == 0:
                    pe.wait_ge(x_loaded[q % 2], 16 * (NK // 2 * b + q // 2 + 1))
                if due(NJ * b + j):
                    pe.wait_ge(x_kept, NJ * b + j)
                for c in range(DC):
                    t = pe.transpose(xT_ps[:, c, :], x_in[:, q % 2, j % 2, c * P:(c + 1) * P], id32[:, :])
                t.then_inc(x_turned, 1)

            def project(b, j):
                pe.wait_ge(x_kept, NJ * b + j + 1)
                if due(2 * (NJ * b + j)):
                    pe.wait_ge(wh_kept, 2 * (NJ * b + j))
                if j == 0:
                    if due(b):
                        pe.wait_ge(fold_made, b)
                for c in range(DC):
                    t = pe.matmul(wh_ps[:, 0:WC], xT[:, j % 2, c, :], w_aug[:, c, :],
                                  start=(c == 0), stop=(c == DC - 1))
                t.then_inc(wh_made, 1)

            def turn_s(b):
                pe.wait_ge(wh_kept, 2 * NJ * (b + 1))
                if due(b):
                    pe.wait_ge(s_kept, b)
                for e in range(2):
                    t = pe.transpose(sT_ps[:, e, :], sd[:, 0:H, :, e].rearrange("p h k -> p (h k)"), id32[:, :])
                t.then_inc(s_turned, 1)

            def mean(b):
                pe.wait_ge(wh_added, NADD * (b + 1))
                for t in range(2):
                    m = pe.matmul(wh_ps[:, 0:H * F], mean_w[:, :], wh_sum[:, t, :, :].rearrange("p h f -> p (h f)"),
                                  start=(t == 0), stop=(t == 1))
                m.then_inc(mean_made, 1)

            def row_tile(b, k, t):
                h = k % H
                m = NP * (UB * b + k) + t // 2
                if t == 0:
                    pe.wait_ge(masks_made, 2 * NCH * (UB * b + k + 1))
                    pe.wait_ge(values_made, 4 * (H * b + h + 1))
                if t % 2 == 0:
                    if due(m - 1):
                        pe.wait_ge(sums_kept, m - 1)
                    apart(pe)
                for g, mask in enumerate((pos, neg)):
                    rows = mask[:, k % 2, :, :].rearrange("p k (q n r e) -> p k q r e n", n=P, r=2, e=2)
                    for j in range(NJ):
                        i = pe.matmul(acc[:, t % 4, 2 * C * g:2 * C * (g + 1)],
                                      rows[:, j // 2, t // 2, t % 2, j % 2, :].bitcast(F8),
                                      values[:, h, j, g, :], start=(j == 0), stop=(j == NJ - 1))
                if t % 2:
                    i.then_inc(sums_made, 1)

            pe.wait_ge(consts_made, NCONST)
            pe.wait_ge(waug_made, 4 * DC)
            for j in range(NJ):
                turn_x(0, j)
                project(0, j)
                if j % 2:
                    turn_adj(j // 2, j // 2 % 2)
            for n in range(NI, NI + 2):
                turn_adj(n, n % 2)
            turn_s(0)
            mean(0)

            def slot(b, k, first, last):
                tiles = list(X_TILES.get(k, ())) if not last else []
                for t in range(NI):
                    if 0 < t <= len(tiles):
                        project(b + 1, tiles[t - 1])
                    if t < len(tiles):
                        turn_x(b + 1, tiles[t])
                    if t == 1 and k == UB - 2 and not last:
                        turn_s(b + 1)
                    if t == 3 and k == UB - 1 and not last:
                        mean(b + 1)
                    row_tile(b, k, t)
                    if t in (1, 5) and (not last or k < H - 1):
                        n = 2 * NI * b + 2 * k + NI + 2 + (t == 5)
                        turn_adj(n, int(t == 5))

            def body(b, first, last):
                for k in range(UB):
                    slot(b, k, first, last)

            batches(pe, body)


_INS = ['x', 'adj', 'L0_gnn_W', 'L0_gnn_a_src', 'L0_gnn_a_dst']


def kernel(**inputs):
    import numpy as _np
    import concourse.bacc as _bacc
    from concourse import mybir as _mybir
    from concourse.bass_utils import run_bass_kernel_spmd as _run

    nc = _bacc.Bacc("TRN2", target_bir_lowering=False, num_devices=1, dynamic_dma_scratch_size=2048)
    arrays, args = {}, []
    for name in _INS:
        a = _np.ascontiguousarray(inputs[name])
        arrays[f"in_{name}_dram"] = a
        args.append(nc.dram_tensor(f"in_{name}_dram", a.shape, _mybir.dt.from_np(a.dtype), kind="ExternalInput").ap())
    shape = inputs['x'].shape
    args.append(nc.dram_tensor("out_0_dram", shape, _mybir.dt.float32, kind="ExternalOutput").ap())
    gat_resnorm(nc, *args)
    r = _run(nc, [arrays], core_ids=[0])
    return r.results[0]["out_0_dram"]
```

```python
import numpy as np
import concourse.bass as bass
from concourse import mybir
from contextlib import ExitStack

F32, F16, BF16 = mybir.dt.float32, mybir.dt.float16, mybir.dt.bfloat16
F8, I32, U8 = mybir.dt.float8e4, mybir.dt.int32, mybir.dt.uint8
ALU, ACT, AX = mybir.AluOpType, mybir.ActivationFunctionType, mybir.AxisListType

ON_SCALAR = (4, 3, 3, 3)


def gat_resnorm(nc, x, adj, w, a_src, a_dst, out):
    B, N, D = x.shape
    H, F = a_src.shape
    P = 128
    NK = N // (2 * P)
    NJ = 2 * NK
    HALF = N // 2
    NI = HALF // P
    C = F + 1
    UB = 2 * H
    NCH = NK // 2
    NP = NI // 2
    DC = D // P
    WC = D + 2 * H
    SLOPE = 0.2
    ONE = 8
    BIG = float(2.0 ** 100)
    VSCALE = float(2.0 ** 14)
    TINY = float(2.0 ** -80)
    ONES = ONE * 0x01010101

    x_pairs = x.rearrange("b (k p e) d -> b k p e d", p=P, e=2)
    out_pairs = out.rearrange("b (k p e) d -> b k p e d", p=P, e=2)
    adj_tiles = adj.rearrange("b (t p) j -> (b t) p j", p=P)
    s_rows = nc.dram_tensor("s_rows", (B, H, N), F32).ap()

    ctx = ExitStack()
    with ctx:
        def sb(name, shape, dt):
            return ctx.enter_context(nc.sbuf_tensor(name, shape, dt))

        def pb(name, shape, dt):
            return ctx.enter_context(nc.psum_tensor(name, shape, dt))

        def sem(name):
            return ctx.enter_context(nc.semaphore(name))

        pos = sb("pos", [P, 2, NK, 2 * HALF], U8)
        neg = sb("neg", [P, 2, NK, 2 * HALF], U8)
        sign = sb("sign", [P, 2, 2, 2 * HALF], U8)
        adjT = sb("adjT", [P, 2, NK, 2 * HALF], U8)
        adj_in = sb("adj_in", [P, 2, N // 2], I32)
        adj_code = sb("adj_code", [P, 2, N], U8)
        values = sb("values", [P, H, NJ, 2, 2 * C], F16)
        wh = sb("wh", [P, NJ, H, C], F32)
        sd = sb("sd", [P, 2 * H, NK, 2], F32)
        s_bc = sb("s_bc", [P, 2, HALF], F32)
        x_in = sb("x_in", [P, 2, 2, D], F32)
        xT = sb("xT", [P, 2, DC, P], F32)
        w_aug = sb("w_aug", [P, DC, WC], F32)
        sums = sb("sums", [P, 2, 2, 2, 2 * C], F32)
        part = sb("part", [P, 2, 2, C], F32)
        row = sb("row", [P, 2, NI, C], F32)
        heads = sb("heads", [P, 2, NI, H * F], F32)
        resid = sb("resid", [P, 2, 2, D], F32)
        expo = sb("expo", [P, 2, D], F32)
        scaled = sb("scaled", [P, NK, C], F32)
        mean_w = sb("mean_w", [P, P], F32)
        id32 = sb("id32", [P, P], F32)
        id16 = sb("id16", [P, P], BF16)
        ones = sb("ones", [P, NJ * H], F32)
        neg_d = sb("neg_d", [P, H, NK, 2], F32)
        big_d = sb("big_d", [P, H, NK, 2], F32)
        shifted = sb("shifted", [P, H, NJ], F32)
        above = sb("above", [P, 3, H, NJ], F32)
        edge = sb("edge", [P, 2, H, NJ], F32)
        edge_n = sb("edge_n", [P, 2, H, NJ], F32)
        alpha_next = sb("alpha_next", [P, 2, H, NJ], F32)
        alpha = sb("alpha", [P, 2, H, NJ], F32)
        fold_next = sb("fold_next", [P, H, C], F32)
        fold = sb("fold", [P, H, C], F32)
        small = sb("small", [P, 64], F32)
        top, top_all = small[:, 0:H + 1], small[:, 5:5 + H + 1]
        w_top = small[:, 10:14]
        recip, recip_w = small[:, 14:14 + NI], small[:, 22:22 + NI]
        stats = small[:, 30:42].rearrange("p (t n) -> p t n", t=2)
        moments = small[:, 42:46].rearrange("p (t n) -> p t n", t=2)
        var_eps, rstd, minus_half = small[:, 46:48], small[:, 48:50], small[:, 50:52]
        wh_sum = scaled.rearrange("p k c -> p (k c)")[:, 0:2 * H * F].rearrange("p (t h f) -> p t h f", t=2, h=H)
        top_quarters = small[:, 52:56]
        sT = x_in[0:H * NK, 0, 0, :].rearrange("p (n e) -> p n e", e=2)
        a_bc = values[:, 0, :, :, :].rearrange("p a b c -> p (a b c)").bitcast(F32)[:, 0:2 * H * F]
        a_prod = values[:, 1, :, :, :].rearrange("p a b c -> p (a b c)").bitcast(F32)[:, 0:H * F]

        acc = pb("acc", [P, 4, 512], F32)
        adj_ps = pb("adj_ps", [P, NK, P], BF16)
        wh_ps = pb("wh_ps", [P, 2, 512], F32)
        x_ps = pb("x_ps", [P, 512], F32)
        xT_ps = x_ps[:, :].rearrange("p (e c n) -> p e c n", e=2, c=DC)
        sT_ps = wh_ps[0:H * NK, 0, 0:2 * P].rearrange("p (e n) -> p e n", e=2)

        waits_passed = sem("waits_passed")
        w_loaded = sem("w_loaded")
        x_loaded = [sem(f"x_loaded{i}") for i in range(2)]
        s_loaded = [sem(f"s_loaded{i}") for i in range(2)]
        resid_loaded = [sem(f"resid_loaded{i}") for i in range(2)]
        adj_loaded = [sem(f"adj_loaded{i}") for i in range(2)]
        s_stored = sem("s_stored")
        out_stored = [sem(f"out_stored{i}") for i in range(2)]
        consts_made = sem("consts_made")
        waug_made = sem("waug_made")
        adj_coded = sem("adj_coded")
        adj_turned = sem("adj_turned")
        adj_kept = sem("adj_kept")
        x_turned = sem("x_turned")
        x_kept = sem("x_kept")
        wh_made = sem("wh_made")
        wh_kept = sem("wh_kept")
        s_turned = sem("s_turned")
        s_kept = sem("s_kept")
        d_flipped = sem("d_flipped")
        big_made = sem("big_made")
        scalar_signs = sem("scalar_signs")
        vector_signs = sem("vector_signs")
        masks_made = sem("masks_made")
        sums_made = sem("sums_made")
        sums_kept = sem("sums_kept")
        sums_read = sem("sums_read")
        part_steps = sem("part_steps")
        recip_made = sem("recip_made")
        heads_made = sem("heads_made")
        values_scaled = sem("values_scaled")
        highs_made = sem("highs_made")
        values_made = sem("values_made")
        tops_made = sem("tops_made")
        tops_shared = sem("tops_shared")
        factor_steps = sem("factor_steps")
        exps_made = sem("exps_made")
        wh_added = sem("wh_added")
        mean_made = sem("mean_made")
        fold_made = sem("fold_made")
        latched = sem("latched")
        wtop_latched = sem("wtop_latched")
        elu_exp = sem("elu_exp")
        norm_steps = sem("norm_steps")
        rstd_made = sem("rstd_made")
        out_made = sem("out_made")

        NCONST = 9
        LEAD = 1
        VECTOR_FINISH = (0, 1, 7)
        NT = 6
        NF = 9
        NS = 7
        NADD = NJ // 2 - 1

        TOPS_AT = [(4, 0), (4, 2), (5, 0), (5, 2)]

        def due(count):
            return not isinstance(count, int) or count > 0

        def apart(eng):
            eng.sem_inc(waits_passed, 1)

        def batches(eng, body):
            body(0, True, False)
            with eng.Fori(1, B - 1) as b:
                body(b, False, False)
            body(B - 1, False, True)

        X_START = NI * 2 + 2

        def x_step(q):
            return 3 * q

        def x_pairs_at(k, t, later):
            return [q for q in range(NK) if x_step(q) + later == NI * k + t - X_START]

        V_START = NCH * (UB - 2) + 2

        V_BEFORE = NCH * UB - V_START

        def value_step_at(b, k, c, last):
            if k < H:
                n = NCH * (UB + k) + c - V_START
                return None if n >= 4 * H else (b, n // 4, n % 4)
            n = NCH * k + c - V_START
            return None if last or n < 0 else (b + 1, n // 4, n % 4)

        X_LOADS = [(1, 1), (1, 3), (2, 1), (2, 2), (3, 0), (3, 2), (4, 0), (4, 1)]

        def finish_heads(eng, b, k):
            half, h = k // H, k % H
            u = UB * b + k
            eng.wait_ge(recip_made, 2 * (u + 1))
            if due(2 * (UB * b + half * H - H)):
                eng.wait_ge(out_made, 2 * (UB * b + half * H - H))
            eng.tensor_tensor(heads[:, half, :, h * F:(h + 1) * F], row[:, k % 2, :, 0:F],
                              recip_w[:, :].unsqueeze(2).to_broadcast([P, NI, F]), ALU.mult
                              ).then_inc(heads_made, 1)
            eng.wait_ge(heads_made, u + 1)

        block = ctx.enter_context(nc.Block())

        @block.sync
        def _(sp):
            def load_x(b, q):
                if due(NK * b + q - 1):
                    sp.wait_ge(x_turned, NK * b + q - 1)
                apart(sp)
                if q == 0:
                    if due(16 * b):
                        sp.wait_ge(s_stored, 16 * b)
                apart(sp)
                sp.dma_start(x_in[:, q % 2, :, :], x_pairs[b, q, :, :, :]).then_inc(x_loaded[q % 2], 16)

            def load_s(b, k):
                u = UB * b + k
                if k == 0:
                    sp.wait_ge(s_stored, 16 * (b + 1))
                    apart(sp)
                if due(NCH * (u - 1)):
                    sp.wait_ge(scalar_signs, NCH * (u - 1))
                apart(sp)
                if due((4 * NCH - sum(ON_SCALAR)) * (u - 1)):
                    sp.wait_ge(vector_signs, (4 * NCH - sum(ON_SCALAR)) * (u - 1))
                apart(sp)
                half, h = k // H, k % H
                sp.dma_start(s_bc[:, k % 2, :],
                             s_rows[b, h:h + 1, half * HALF:(half + 1) * HALF].to_broadcast([P, HALF])
                             ).then_inc(s_loaded[k % 2], 16)

            def store_s(b):
                sp.wait_ge(s_kept, b + 1)
                apart(sp)
                sp.dma_start(s_rows[b, :, :].rearrange("h (k n) -> (h k) n", k=NK),
                             x_in[0:H * NK, 0, 0, :]).then_inc(s_stored, 16)

            def load_resid(b, k):
                if due(8 * (UB * b + k - k % 2)):
                    sp.wait_ge(out_stored[k % 2], 8 * (UB * b + k - k % 2))
                apart(sp)
                sp.dma_start(resid[:, k % 2, :, :], x_pairs[b, k, :, :, :]).then_inc(resid_loaded[k % 2], 16)

            def store_out(b, k):
                r = UB * b + k
                sp.wait_ge(out_made, 2 * (r + 1))
                apart(sp)
                sp.dma_start(out_pairs[b, k, :, :, :], resid[:, k % 2, :, :]).then_inc(out_stored[k % 2], 16)

            for c in range(DC):
                sp.dma_start(w_aug[:, c, 0:D], w[c * P:(c + 1) * P, :]).then_inc(w_loaded, 16)
            for i, a in enumerate((a_src, a_dst)):
                sp.dma_start(a_bc[:, i * H * F:(i + 1) * H * F],
                             a.rearrange("(o h) f -> o (h f)", o=1).to_broadcast([P, H * F])
                             ).then_inc(w_loaded, 16)
            def load_adj(n, i):
                if due(2 * (n - 1) + i + 1):
                    sp.wait_ge(adj_coded, 2 * (n - 1) + i + 1)
                apart(sp)
                sp.dma_start(adj_in[:, i, :], adj_tiles[n, :, i * (N // 2):(i + 1) * (N // 2)]
                             ).then_inc(adj_loaded[i], 16)

            for q in range(NK):
                load_x(0, q)
                load_adj(q, 0)
                load_adj(q, 1)
            store_s(0)
            load_s(0, 0)
            load_s(0, 1)
            for n in range(NI, NI + 4):
                load_adj(n, 0)
                load_adj(n, 1)
            load_adj(NI + 4, 0)

            def slot(b, k, first, last):
                if k < UB - 2:
                    load_s(b, k + 2)
                elif not last:
                    load_s(b + 1, k + 2 - UB)
                if not (first and k < 6):
                    store_out(b if k >= 6 else b - 1, (k - 6) % UB)
                if not (first and k < 4):
                    load_resid(b if k >= 4 else b - 1, (k - 4) % UB)
                for c in range(NCH):
                    n = 2 * k + NI + 4 + (c + 1) // 2
                    if not last or n < 2 * NI:
                        load_adj(2 * NI * b + n, (c + 1) % 2)
                    if not last and (k, c) in X_LOADS:
                        load_x(b + 1, X_LOADS.index((k, c)))
                if k == UB - 3 and not last:
                    store_s(b + 1)

            def body(b, first, last):
                for k in range(UB):
                    slot(b, k, first, last)

            batches(sp, body)
            for k in range(2, UB):
                store_out(B - 1, k)
                if k + 2 < UB:
                    load_resid(B - 1, k + 2)
            for i in range(2):
                sp.wait_ge(out_stored[i], 16 * UB * B // 2)

        @block.gpsimd
        def _(pool):
            def scale_values(b, h, i):
                g, t0 = i // 2, (i % 2) * NK
                step = 4 * (H * b + h) + i
                if i == 0:
                    pool.wait_ge(factor_steps, NF * (b + 1))
                if i == 0 and h == 0:
                    pool.wait_ge(mean_made, b + 1)
                if due(step):
                    pool.wait_ge(values_made, step)
                pool.tensor_tensor(scaled[:, :, :], wh[:, t0:t0 + NK, h, :],
                                   edge_n[:, g, h, t0:t0 + NK].unsqueeze(2).to_broadcast([P, NK, C]),
                                   ALU.mult).then_inc(values_scaled, 1)

            def low_values(b, h, i):
                g, t0 = i // 2, (i % 2) * NK
                step = 4 * (H * b + h) + i
                pool.wait_ge(highs_made, step + 1)
                pool.tensor_tensor(values[:, h, t0:t0 + NK, g, C:2 * C], scaled[:, :, :],
                                   values[:, h, t0:t0 + NK, g, 0:C], ALU.subtract).then_inc(values_made, 1)

            def share_tops(b):
                pool.wait_ge(tops_made, NT * (b + 1))
                apart(pool)
                pool.partition_all_reduce(top_all[:, :], top[:, :], P, bass.bass_isa.ReduceOp.max
                                          ).then_inc(tops_shared, 1)

            def add_wh(b, adds):
                for i in adds:
                    a = wh[:, 0:2, :, 0:F] if i == 0 else wh_sum[:, :, :, :]
                    pool.wait_ge(wh_kept, 2 * (NK * b + i + 2))
                    if i == 0:
                        if due(4 * H * b):
                            pool.wait_ge(values_made, 4 * H * b)
                    if due(NADD * b + i):
                        pool.wait_ge(wh_added, NADD * b + i)
                    pool.tensor_tensor(wh_sum[:, :, :, :], a, wh[:, 2 * i + 2:2 * i + 4, :, 0:F],
                                       ALU.add).then_inc(wh_added, 1)

            def latch(b):
                pool.wait_ge(exps_made, 4 * (b + 1))
                pool.wait_ge(fold_made, b + 1)
                if due(3 * NP * UB * b):
                    pool.wait_ge(part_steps, 3 * NP * UB * b)
                apart(pool)
                pool.tensor_scalar(alpha[:, :, :, :], alpha_next[:, :, :, :], 1.0, 0.0, ALU.mult, ALU.add
                                   ).then_inc(latched, 1)
                pool.tensor_scalar(fold[:, :, :], fold_next[:, :, :], 1.0, 0.0, ALU.mult, ALU.add
                                   ).then_inc(latched, 1)
                pool.wait_ge(latched, 2 * (b + 1))

            def epilogue(b, k, c):
                half, h, i = k // H, k % H, c % 2
                m = NP * (UB * b + k) + c
                t0 = half * NI + 2 * c
                s = sums[:, i, :, :, :]
                pool.wait_ge(sums_kept, m + 1)
                if c == 0:
                    if due(UB * b + k - 1):
                        pool.wait_ge(heads_made, UB * b + k - 1)
                if due(3 * m):
                    pool.wait_ge(part_steps, 3 * m)
                pool.tensor_tensor(part[:, :, :, :], s[:, :, :, 0:C], s[:, :, :, C:2 * C], ALU.add
                                   ).then_inc(sums_read, 1)
                pool.wait_ge(sums_read, m + 1)
                al = alpha[:, :, h, t0:t0 + 2].rearrange("p g t -> p t g").unsqueeze(3)
                pool.tensor_tensor(part[:, :, :, :], part[:, :, :, :], al.to_broadcast([P, 2, 2, C]),
                                   ALU.mult).then_inc(part_steps, 1)
                pool.wait_ge(part_steps, 3 * m + 1)
                r = row[:, k % 2, 2 * c:2 * c + 2, :]
                pool.tensor_tensor(r, part[:, :, 0, :], part[:, :, 1, :], ALU.add).then_inc(part_steps, 1)
                pool.wait_ge(part_steps, 3 * m + 2)
                pool.tensor_tensor(r, r, fold[:, h, :].unsqueeze(1).to_broadcast([P, 2, C]), ALU.add
                                   ).then_inc(part_steps, 1)

            def inv_std(b, k):
                r = UB * b + k
                pool.wait_ge(norm_steps, NS * (r + 1))
                pool.tensor_tensor(rstd[:, :], var_eps[:, :], minus_half[:, :], ALU.pow).then_inc(rstd_made, 1)

            for ident in (id32, id16):
                pool.memset(ident[:, :], 0.0).then_inc(consts_made, 1)
            pool.memset(mean_w[:, :], TINY / N).then_inc(consts_made, 1)
            pool.memset(minus_half[:, :], -0.5).then_inc(consts_made, 1)
            pool.memset(ones[:, :], 1.0).then_inc(consts_made, 1)
            pool.memset(fold_next[:, :, :], TINY).then_inc(consts_made, 1)
            pool.memset(wh[:, :, :, F:C], 1.0).then_inc(consts_made, 1)
            pool.wait_ge(consts_made, NCONST - 2)
            for ident in (id32, id16):
                pool.affine_select(out=ident[:, :], in_=ident[:, :], compare_op=ALU.not_equal, fill=1.0, base=0,
                                   pattern=[[-1, P]], channel_multiplier=1).then_inc(consts_made, 1)
            add_wh(0, range(NADD))
            share_tops(0)
            for n in range(V_BEFORE):
                scale_values(0, n // 4, n % 4)
                low_values(0, n // 4, n % 4)

            def slot(b, k, first, last):
                if k == 0:
                    latch(b)
                for c in range(NP):
                    v = value_step_at(b, k, c, last)
                    if v:
                        scale_values(*v)
                    if k == UB - 3 and c == 3 and not last:
                        share_tops(b + 1)
                    epilogue(b, k, c)
                    if v:
                        low_values(*v)
                    if c == 1 and not (first and k == 0) and k not in VECTOR_FINISH:
                        finish_heads(pool, b if k else b - 1, (k - 1) % UB)
                    if c == 2 and not (first and k < 5):
                        inv_std(b if k >= 5 else b - 1, (k - 5) % UB)
                    if not last:
                        adds = {(4, 0): (0, 1), (4, 1): (2,), (4, 2): (3,), (4, 3): (4,), (5, 1): (5,), (5, 2): (6,)}.get((k, c), ())
                        add_wh(b + 1, adds)

            def body(b, first, last):
                for k in range(UB):
                    slot(b, k, first, last)

            batches(pool, body)
            finish_heads(pool, B - 1, UB - 1)
            for k in range(3, UB):
                inv_std(B - 1, k)

        @block.scalar
        def _(act):
            def keep_xT(b, q):
                act.wait_ge(x_turned, NK * b + q + 1)
                if due(NK * b + q):
                    act.wait_ge(wh_made, NK * b + q)
                act.activation(xT[:, :, :, :], xT_ps, ACT.Copy).then_inc(x_kept, 1)

            def keep_wh(b, q):
                act.wait_ge(wh_made, NK * b + q + 1)
                if q == 0:
                    if due(4 * H * b):
                        act.wait_ge(values_made, 4 * H * b)
                    if due(NADD * b):
                        act.wait_ge(wh_added, NADD * b)
                    if due(NF * b):
                        act.wait_ge(factor_steps, NF * b)
                    if due(b):
                        act.wait_ge(d_flipped, b)
                    if due(b):
                        act.wait_ge(s_turned, b)
                act.activation(wh[:, 2 * q:2 * q + 2, :, 0:F],
                               wh_ps[:, :, 0:D].rearrange("p e (h f) -> p e h f", h=H), ACT.Copy
                               ).then_inc(wh_kept, 1)
                act.activation(sd[:, :, q, :], wh_ps[:, :, D:WC].rearrange("p e c -> p c e"), ACT.Copy
                               ).then_inc(wh_kept, 1)

            def factor_exps(b):
                def f(n):
                    act.wait_ge(factor_steps, NF * b + n)
                if due(2 * b):
                    act.wait_ge(latched, 2 * b)
                f(4)
                act.activation(edge[:, 0, :, :], shifted[:, :, :], ACT.Exp).then_inc(exps_made, 1)
                act.activation(edge[:, 1, :, :], shifted[:, :, :], ACT.Exp, scale=SLOPE).then_inc(exps_made, 1)
                f(7)
                act.activation(alpha_next[:, 0, :, :], above[:, 1, :, :], ACT.Exp, scale=1 - SLOPE
                               ).then_inc(exps_made, 1)
                act.activation(alpha_next[:, 1, :, :], above[:, 2, :, :], ACT.Exp, scale=SLOPE - 1
                               ).then_inc(exps_made, 1)

            def make_big(b):
                act.wait_ge(wh_kept, 2 * NK * (b + 1))
                if due(NCH * UB * b):
                    act.wait_ge(scalar_signs, NCH * UB * b)
                act.activation(big_d[:, :, :, :], sd[:, H:2 * H, :, :], ACT.Copy, scale=BIG).then_inc(big_made, 1)
                act.wait_ge(big_made, b + 1)

            def signs(b, k, c):
                h = k % H
                m = NCH * (UB * b + k) + c
                if c == 0:
                    act.wait_ge(s_loaded[k % 2], 8 * (UB * b + k - k % 2) + 16)
                if due(2 * (m - 1)):
                    act.wait_ge(masks_made, 2 * (m - 1))
                apart(act)
                for i in range(ON_SCALAR[c]):
                    kk, e = i // 2, i % 2
                    a = act.activation(sign[:, c % 2, kk, e:2 * HALF:2].bitcast(F8), s_bc[:, k % 2, :], ACT.Relu,
                                       bias=big_d[:, h, 2 * c + kk, e:e + 1], scale=BIG, saturate=False)
                a.then_inc(scalar_signs, 1)

            def keep_sums(b, k, c):
                m = NP * (UB * b + k) + c
                bank = (2 * c) % 4
                act.wait_ge(sums_made, m + 1)
                if due(m - 1):
                    act.wait_ge(sums_read, m - 1)
                act.activation(sums[:, c % 2, :, :, :].rearrange("p t g n -> p t (g n)"),
                               acc[:, bank:bank + 2, 0:4 * C], ACT.Copy).then_inc(sums_kept, 1)

            def elu_part(b, k):
                half, c, r = k // H, k % H, UB * b + k
                act.wait_ge(heads_made, UB * b + (half + 1) * H)
                if due(NS * (r - 1) + 2):
                    act.wait_ge(norm_steps, NS * (r - 1) + 2)
                act.activation(expo[:, :, :], heads[:, half, 2 * c:2 * c + 2, :], ACT.Exp).then_inc(elu_exp, 1)

            def high_values(b, h, i):
                g, t0 = i // 2, (i % 2) * NK
                step = 4 * (H * b + h) + i
                act.wait_ge(values_scaled, step + 1)
                if i == 0:
                    if due(NP * (UB * b - H + h + 1)):
                        act.wait_ge(sums_made, NP * (UB * b - H + h + 1))
                act.activation(values[:, h, t0:t0 + NK, g, 0:C], scaled[:, :, :], ACT.Copy).then_inc(highs_made, 1)

            for q in range(NK):
                keep_xT(0, q)
                keep_wh(0, q)
            make_big(0)
            signs(0, 0, 0)
            factor_exps(0)
            for n in range(V_BEFORE):
                high_values(0, n // 4, n % 4)
                if n % 2:
                    signs(0, 0, (n + 1) // 2)
            for c in range(LEAD):
                signs(0, 1, c)

            def slot(b, k, first, last):
                for c in range(NCH):
                    if not last:
                        for t in (2 * c, 2 * c + 1):
                            for q in x_pairs_at(k, t, 4):
                                keep_wh(b + 1, q)
                            for q in x_pairs_at(k, t, 1):
                                keep_xT(b + 1, q)
                    ahead = k + 1 + (c + LEAD) // NCH
                    if ahead == UB and c + LEAD == NCH and not last:
                        make_big(b + 1)
                    if ahead < UB:
                        signs(b, ahead, (c + LEAD) % NCH)
                    elif not last:
                        signs(b + 1, ahead - UB, (c + LEAD) % NCH)
                    v = value_step_at(b, k, c, last)
                    keep_sums(b, k, c)
                    if v:
                        high_values(*v)
                    if c == 0 and k == UB - 2 and not last:
                        factor_exps(b + 1)
                    if c == 3 and not (first and k < 4):
                        elu_part(b if k >= 4 else b - 1, (k - 4) % UB)

            def body(b, first, last):
                for k in range(UB):
                    slot(b, k, first, last)

            batches(act, body)
            for k in range(4, UB):
                elu_part(B - 1, k)

        @block.vector
        def _(dve):
            def code_adj(n, i, half):
                dve.wait_ge(adj_loaded[half], 16 * (n + 1))
                if half == 0:
                    if due(n - 1):
                        dve.wait_ge(adj_turned, n - 1)
                dve.tensor_scalar(adj_code[:, i, half * (N // 2):(half + 1) * (N // 2)], adj_in[:, half, :],
                                  0.0, float(ONE - 1), ALU.is_gt, ALU.add).then_inc(adj_coded, 1)

            def keep_adj(n, g, half, t):
                dve.wait_ge(adj_turned, n + 1)
                if due(2 * NCH * H * (g - 1)):
                    dve.wait_ge(masks_made, 2 * NCH * H * (g - 1))
                dve.tensor_copy(adjT[:, half, :, 2 * t * P:2 * (t + 1) * P].bitcast(I32),
                                adj_ps[:, :, :].bitcast(I32)).then_inc(adj_kept, 1)

            def keep_s(b):
                dve.wait_ge(s_turned, b + 1)
                dve.wait_ge(x_turned, NK * (b + 1))
                dve.tensor_copy(sT.rearrange("p n e -> p e n"), sT_ps).then_inc(s_kept, 1)

            def tops(b, i):
                n = NJ // 4
                done = NT * b + i
                dve.wait_ge(wh_kept, 2 * (NK * b + (i + 1) * n // 2))
                if i == 0:
                    if due(b):
                        dve.wait_ge(tops_shared, b)
                dve.tensor_reduce(top_quarters[:, i:i + 1], wh[:, i * n:(i + 1) * n, :, 0:F], AX.XYZ, ALU.max,
                                  apply_absolute_value=True).then_inc(tops_made, 1)
                if i == 3:
                    dve.tensor_reduce(top[:, 0:H], sd[:, H:2 * H, :, :], AX.XY, ALU.max).then_inc(tops_made, 1)
                    dve.wait_ge(tops_made, done + 2)
                    dve.tensor_reduce(top[:, H:H + 1], top_quarters, AX.X, ALU.max).then_inc(tops_made, 1)

            def factors(b):
                n = [0]

                def step(ins):
                    n[0] += 1
                    ins.then_inc(factor_steps, 1)
                    dve.wait_ge(factor_steps, NF * b + n[0])

                s = sd[:, 0:H, :, :].rearrange("p h k e -> p h (k e)")
                d = sd[:, H:2 * H, :, :].rearrange("p h k e -> p h (k e)")
                D_bc = top_all[:, 0:H].unsqueeze(2).to_broadcast([P, H, NJ])
                dve.wait_ge(tops_shared, b + 1)
                if due(b):
                    dve.wait_ge(wtop_latched, b)
                step(dve.tensor_scalar(w_top[:, 0:1], top_all[:, H:H + 1], 1e-30, None, ALU.max))
                step(dve.reciprocal(w_top[:, 1:2], w_top[:, 0:1]))
                step(dve.tensor_scalar(w_top[:, 2:3], w_top[:, 1:2], VSCALE, None, ALU.mult))
                step(dve.tensor_tensor(shifted[:, :, :], d, D_bc, ALU.subtract))
                step(dve.tensor_tensor(above[:, 0, :, :], s, D_bc, ALU.add))
                step(dve.tensor_scalar(above[:, 1, :, :], above[:, 0, :, :], 0.0, None, ALU.min))
                step(dve.tensor_scalar(above[:, 2, :, :], above[:, 0, :, :], 0.0, None, ALU.max))

            def factors_end(b):
                dve.tensor_scalar(wh[:, :, :, F], ones[:, :].rearrange("p (j h) -> p j h", h=H), w_top[:, 0:1], None,
                                  ALU.mult).then_inc(factor_steps, 1)
                dve.wait_ge(exps_made, 4 * b + 2)
                if due(4 * H * b):
                    dve.wait_ge(values_made, 4 * H * b)
                dve.tensor_scalar(edge_n[:, :, :, :], edge[:, :, :, :], w_top[:, 2:3], None, ALU.mult
                                  ).then_inc(factor_steps, 1)

            def make_fold(b):
                dve.wait_ge(mean_made, b + 1)
                if due(2 * b):
                    dve.wait_ge(latched, 2 * b)
                dve.tensor_scalar(fold_next[:, :, 0:F], wh_ps[:, 1, 0:H * F].rearrange("p (h f) -> p h f", h=H),
                                  w_top[:, 1:2], None, ALU.mult).then_inc(fold_made, 1)

            def flip_d(b):
                if due((4 * NCH - sum(ON_SCALAR)) * UB * b):
                    dve.wait_ge(vector_signs, (4 * NCH - sum(ON_SCALAR)) * UB * b)
                dve.tensor_scalar(neg_d[:, :, :, :], sd[:, H:2 * H, :, :], -1.0, None, ALU.mult
                                  ).then_inc(d_flipped, 1)
                dve.wait_ge(d_flipped, b + 1)

            def signs(b, k, c):
                h = k % H
                m = NCH * (UB * b + k) + c
                if c == 0:
                    dve.wait_ge(s_loaded[k % 2], 8 * (UB * b + k - k % 2) + 16)
                for i in range(ON_SCALAR[c], 4):
                    kk, e = i // 2, i % 2
                    if due(2 * (m - 1)):
                        dve.wait_ge(masks_made, 2 * (m - 1))
                    dve.tensor_scalar(sign[:, c % 2, kk, e:2 * HALF:2], s_bc[:, k % 2, :],
                                      neg_d[:, h, 2 * c + kk, e:e + 1], float(ONE), ALU.is_gt, ALU.mult
                                      ).then_inc(vector_signs, 1)

            def masks(b, k, c):
                half, u = k // H, UB * b + k
                m = NCH * u + c
                per_unit = 4 * NCH - sum(ON_SCALAR)
                if c == 0:
                    dve.wait_ge(adj_kept, NI * (2 * b + half + 1))
                    if due(NP * (u - 1)):
                        dve.wait_ge(sums_made, NP * (u - 1))
                dve.wait_ge(scalar_signs, m + 1)
                if due(per_unit * u + sum(4 - n for n in ON_SCALAR[0:c + 1])):
                    dve.wait_ge(vector_signs, per_unit * u + sum(4 - n for n in ON_SCALAR[0:c + 1]))

                def words(t):
                    return t.rearrange("p k n -> p (k n)").bitcast(I32)
                sg = words(sign[:, c % 2, :, :])
                ad = words(adjT[:, half, 2 * c:2 * c + 2, :])
                dve.tensor_tensor(words(pos[:, k % 2, 2 * c:2 * c + 2, :]), sg, ad, ALU.bitwise_and
                                  ).then_inc(masks_made, 1)
                dve.scalar_tensor_tensor(words(neg[:, k % 2, 2 * c:2 * c + 2, :]), sg, ONES, ad,
                                         ALU.bitwise_xor, ALU.bitwise_and).then_inc(masks_made, 1)

            def make_recip(b, k):
                u = UB * b + k
                dve.wait_ge(part_steps, 3 * NP * (u + 1))
                if due(u):
                    dve.wait_ge(heads_made, u)
                dve.reciprocal(recip[:, :], row[:, k % 2, :, F]).then_inc(recip_made, 1)
                dve.wait_ge(recip_made, 2 * u + 1)
                dve.tensor_scalar(recip_w[:, :], recip[:, :], w_top[:, 3:4], None, ALU.mult).then_inc(recip_made, 1)

            def latch_top(b):
                dve.wait_ge(factor_steps, NF * b + 1)
                if due(2 * UB * b):
                    dve.wait_ge(recip_made, 2 * UB * b)
                dve.tensor_copy(w_top[:, 3:4], w_top[:, 0:1]).then_inc(wtop_latched, 1)
                dve.wait_ge(wtop_latched, b + 1)

            def norm_start(b, k):
                half, c, i, r = k // H, k % H, k % 2, UB * b + k
                n = [0]

                def step(ins):
                    n[0] += 1
                    ins.then_inc(norm_steps, 1)

                dve.wait_ge(elu_exp, r + 1)
                dve.wait_ge(resid_loaded[i], 8 * (UB * b + k - i) + 16)
                res = resid[:, i, :, :]
                step(dve.scalar_tensor_tensor(expo[:, :, :], expo[:, :, :], 1.0, res, ALU.min, ALU.add))
                dve.wait_ge(norm_steps, NS * r + 1)
                step(dve.scalar_tensor_tensor(res, heads[:, half, 2 * c:2 * c + 2, :], 0.0, expo[:, :, :],
                                              ALU.max, ALU.add))
                dve.wait_ge(norm_steps, NS * r + 2)
                for t in range(2):
                    step(dve.bn_stats(stats[:, t, :], resid[:, i, t, :]))
                dve.wait_ge(norm_steps, NS * r + 4)
                apart(dve)
                for t in range(2):
                    step(dve.bn_aggr(moments[:, t, :], stats[:, t, :]))
                dve.wait_ge(norm_steps, NS * r + 6)
                if due(r):
                    dve.wait_ge(rstd_made, r)
                step(dve.tensor_scalar(var_eps[:, :], moments[:, :, 1], 1e-5, None, ALU.add))

            def norm_end(b, k):
                i, r = k % 2, UB * b + k
                dve.wait_ge(rstd_made, r + 1)
                for t in range(2):
                    dve.tensor_scalar(resid[:, i, t, :], resid[:, i, t, :], moments[:, t, 0:1], rstd[:, t:t + 1],
                                      ALU.subtract, ALU.mult).then_inc(out_made, 1)
                dve.wait_ge(out_made, 2 * (r + 1))

            dve.wait_ge(w_loaded, 16 * (DC + 2))
            done = 0
            for c in range(DC):
                for i in range(2):
                    if due(done):
                        dve.wait_ge(waug_made, done)
                    dve.tensor_tensor(a_prod, w_aug[:, c, 0:D], a_bc[:, i * D:(i + 1) * D], ALU.mult
                                      ).then_inc(waug_made, 1)
                    dve.wait_ge(waug_made, done + 1)
                    dve.tensor_reduce(w_aug[:, c, D + i * H:D + (i + 1) * H],
                                      a_prod.rearrange("p (h f) -> p h f", h=H), AX.X, ALU.add
                                      ).then_inc(waug_made, 1)
                    done += 2
            for n in range(NI):
                code_adj(n, n % 2, 0)
                code_adj(n, n % 2, 1)
                if n:
                    keep_adj(n - 1, 0, 0, n - 1)
            keep_adj(NI - 1, 0, 0, NI - 1)
            keep_s(0)
            for i in range(4):
                tops(0, i)
            flip_d(0)
            factors(0)
            factors_end(0)
            make_fold(0)
            for c in range(NCH):
                n = NI + c
                if c >= 2:
                    keep_adj(n - 2, 1, 1, c - 2)
                code_adj(n, n % 2, 0)
                if c < NCH - 1:
                    code_adj(n, n % 2, 1)
                signs(0, 0, c)
                masks(0, 0, c)

            def slot(b, k, first, last):
                more = not (last and k == UB - 1)
                nb, nk = (b, k + 1) if k < UB - 1 else (b + 1, 0)
                turn = not last or k < H - 1
                code = not last or k < H - 2
                n0 = 2 * NI * b + 2 * k + NI + 2
                g = 2 * nb + nk // H + 1
                half, t0 = (nk // H + 1) % 2, 2 * (nk % H)
                if k == UB - 1 and more:
                    flip_d(nb)
                for c in range(NCH):
                    if more:
                        signs(nb, nk, c)
                        masks(nb, nk, c)
                    if c == 1 and not (first and k == 0):
                        make_recip(b if k else b - 1, (k - 1) % UB)
                        if k in VECTOR_FINISH:
                            finish_heads(dve, b if k else b - 1, (k - 1) % UB)
                    if c == 1 and k == 0:
                        latch_top(b)
                    if c == 0 and not (first and k < 6):
                        norm_end(b if k >= 6 else b - 1, (k - 6) % UB)
                    if c == 1 and turn:
                        keep_adj(n0, g, half, t0)
                    if c == 3 and turn:
                        keep_adj(n0 + 1, g, half, t0 + 1)
                    if c == 0 and turn:
                        code_adj(n0 + 1, 1, 1)
                    elif c and code:
                        code_adj(n0 + 2 + c // 3, c // 3, int(c == 2))
                    if c == 1 and not (first and k < 5):
                        norm_start(b if k >= 5 else b - 1, (k - 5) % UB)
                    if k == UB - 3 and c == 2 and not last:
                        keep_s(b + 1)
                    if (k, c) in TOPS_AT and not last:
                        tops(b + 1, TOPS_AT.index((k, c)))
                    if k == UB - 2 and not last:
                        if c == 0:
                            factors(b + 1)
                        if c == 1:
                            factors_end(b + 1)
                        if c == 2:
                            make_fold(b + 1)

            def body(b, first, last):
                for k in range(UB):
                    slot(b, k, first, last)

            batches(dve, body)
            make_recip(B - 1, UB - 1)
            norm_end(B - 1, 2)
            for k in range(3, UB):
                norm_start(B - 1, k)
                norm_end(B - 1, k)

        @block.tensor
        def _(pe):
            def turn_adj(n, i):
                pe.wait_ge(adj_coded, 2 * (n + 1))
                if due(n):
                    pe.wait_ge(adj_kept, n)
                for kk in range(NK):
                    t = pe.transpose(adj_ps[:, kk, :],
                                     adj_code[:, i, 2 * P * kk:2 * P * (kk + 1)].bitcast(BF16), id16[:, :])
                t.then_inc(adj_turned, 1)

            def turn_x(b, q):
                pe.wait_ge(x_loaded[q % 2], 16 * (NK // 2 * b + q // 2 + 1))
                if due(NK * b + q):
                    pe.wait_ge(x_kept, NK * b + q)
                for e in range(2):
                    for c in range(DC):
                        t = pe.transpose(xT_ps[:, e, c, :], x_in[:, q % 2, e, c * P:(c + 1) * P], id32[:, :])
                t.then_inc(x_turned, 1)

            def project(b, q):
                pe.wait_ge(x_kept, NK * b + q + 1)
                if due(2 * (NK * b + q)):
                    pe.wait_ge(wh_kept, 2 * (NK * b + q))
                if q == 0:
                    if due(b):
                        pe.wait_ge(fold_made, b)
                for e in range(2):
                    for c in range(DC):
                        t = pe.matmul(wh_ps[:, e, 0:WC], xT[:, e, c, :], w_aug[:, c, :],
                                      start=(c == 0), stop=(c == DC - 1))
                t.then_inc(wh_made, 1)

            def turn_s(b):
                pe.wait_ge(wh_kept, 2 * NK * (b + 1))
                for e in range(2):
                    t = pe.transpose(sT_ps[:, e, :], sd[:, 0:H, :, e].rearrange("p h k -> p (h k)"), id32[:, :])
                t.then_inc(s_turned, 1)

            def mean(b):
                pe.wait_ge(wh_added, NADD * (b + 1))
                for t in range(2):
                    m = pe.matmul(wh_ps[:, 1, 0:H * F], mean_w[:, :], wh_sum[:, t, :, :].rearrange("p h f -> p (h f)"),
                                  start=(t == 0), stop=(t == 1))
                m.then_inc(mean_made, 1)

            def row_tile(b, k, t):
                h = k % H
                m = NP * (UB * b + k) + t // 2
                if t == 0:
                    pe.wait_ge(masks_made, 2 * NCH * (UB * b + k + 1))
                    pe.wait_ge(values_made, 4 * (H * b + h + 1))
                if t % 2 == 0:
                    if due(m - 1):
                        pe.wait_ge(sums_kept, m - 1)
                    apart(pe)
                for g, mask in enumerate((pos, neg)):
                    rows = mask[:, k % 2, :, :].rearrange("p k (q n r e) -> p k q r e n", n=P, r=2, e=2)
                    for j in range(NJ):
                        i = pe.matmul(acc[:, t % 4, 2 * C * g:2 * C * (g + 1)],
                                      rows[:, j // 2, t // 2, t % 2, j % 2, :].bitcast(F8),
                                      values[:, h, j, g, :], start=(j == 0), stop=(j == NJ - 1))
                if t % 2:
                    i.then_inc(sums_made, 1)

            pe.wait_ge(consts_made, NCONST)
            pe.wait_ge(waug_made, 4 * DC)
            for q in range(NK):
                turn_x(0, q)
                project(0, q)
                turn_adj(q, q % 2)
            turn_s(0)
            mean(0)
            for n in range(NI, NI + 2):
                turn_adj(n, n % 2)

            def slot(b, k, first, last):
                for t in range(NI):
                    if not last:
                        for q in x_pairs_at(k, t, 3):
                            project(b + 1, q)
                        for q in x_pairs_at(k, t, 0):
                            turn_x(b + 1, q)
                    if t == 5 and k == UB - 3 and not last:
                        turn_s(b + 1)
                    if t == 1 and k == UB - 2 and not last:
                        mean(b + 1)
                    row_tile(b, k, t)
                    if t in (2, 5) and (not last or k < H - 1):
                        n = 2 * NI * b + 2 * k + NI + 2 + (t == 5)
                        turn_adj(n, int(t == 5))

            def body(b, first, last):
                for k in range(UB):
                    slot(b, k, first, last)

            batches(pe, body)


_INS = ['x', 'adj', 'L0_gnn_W', 'L0_gnn_a_src', 'L0_gnn_a_dst']


def kernel(**inputs):
    import numpy as _np
    import concourse.bacc as _bacc
    from concourse import mybir as _mybir
    from concourse.bass_utils import run_bass_kernel_spmd as _run

    nc = _bacc.Bacc("TRN2", target_bir_lowering=False, num_devices=1, dynamic_dma_scratch_size=2048)
    arrays, args = {}, []
    for name in _INS:
        a = _np.ascontiguousarray(inputs[name])
        arrays[f"in_{name}_dram"] = a
        args.append(nc.dram_tensor(f"in_{name}_dram", a.shape, _mybir.dt.from_np(a.dtype), kind="ExternalInput").ap())
    shape = inputs['x'].shape
    args.append(nc.dram_tensor("out_0_dram", shape, _mybir.dt.float32, kind="ExternalOutput").ap())
    gat_resnorm(nc, *args)
    r = _run(nc, [arrays], core_ids=[0])
    return r.results[0]["out_0_dram"]
```

```python
import numpy as np
import concourse.bass as bass
from concourse import mybir
from contextlib import ExitStack

F32, F16, BF16 = mybir.dt.float32, mybir.dt.float16, mybir.dt.bfloat16
F8, I32, U8 = mybir.dt.float8e4, mybir.dt.int32, mybir.dt.uint8
ALU, ACT, AX = mybir.AluOpType, mybir.ActivationFunctionType, mybir.AxisListType

ON_SCALAR = 4 * ((3, 3, 3, 3),) + 2 * ((3, 3, 3, 4),) + 2 * ((3, 4, 3, 4),)


def gat_resnorm(nc, x, adj, w, a_src, a_dst, out):
    B, N, D = x.shape
    H, F = a_src.shape
    P = 128
    NK = N // (2 * P)
    NJ = 2 * NK
    HALF = N // 2
    NI = HALF // P
    C = F + 1
    UB = 2 * H
    NCH = NK // 2
    NP = NI // 2
    DC = D // P
    WC = D + 2 * H
    SLOPE = 0.2
    ONE = 8
    BIG = float(2.0 ** 100)
    VSCALE = float(2.0 ** 14)
    TINY = float(2.0 ** -80)
    ONES = ONE * 0x01010101

    x_pairs = x.rearrange("b (k p e) d -> b k p e d", p=P, e=2)
    out_pairs = out.rearrange("b (k p e) d -> b k p e d", p=P, e=2)
    adj_tiles = adj.rearrange("b (t p) j -> (b t) p j", p=P)
    s_rows = nc.dram_tensor("s_rows", (B, H, N), F32).ap()

    ctx = ExitStack()
    with ctx:
        def sb(name, shape, dt):
            return ctx.enter_context(nc.sbuf_tensor(name, shape, dt))

        def pb(name, shape, dt):
            return ctx.enter_context(nc.psum_tensor(name, shape, dt))

        def sem(name):
            return ctx.enter_context(nc.semaphore(name))

        pos = sb("pos", [P, 2, NK, 2 * HALF], U8)
        neg = sb("neg", [P, 2, NK, 2 * HALF], U8)
        sign = sb("sign", [P, 2, 2, 2 * HALF], U8)
        adjT = sb("adjT", [P, 2, NK, 2 * HALF], U8)
        adj_in = sb("adj_in", [P, 2, N // 2], I32)
        adj_code = sb("adj_code", [P, 2, N], U8)
        values = sb("values", [P, H, NJ, 2, 2 * C], F16)
        wh = sb("wh", [P, NJ, H, C], F32)
        sd = sb("sd", [P, 2 * H, NK, 2], F32)
        s_bc = sb("s_bc", [P, 2, HALF], F32)
        x_in = sb("x_in", [P, 2, 2, D], F32)
        xT = sb("xT", [P, 2, DC, P], F32)
        w_aug = sb("w_aug", [P, DC, WC], F32)
        sums = sb("sums", [P, 2, 2, 2, 2 * C], F32)
        part = sb("part", [P, 2, 2, C], F32)
        row = sb("row", [P, 2, NI, C], F32)
        heads = sb("heads", [P, 2, NI, H * F], F32)
        resid = sb("resid", [P, 2, 2, D], F32)
        expo = sb("expo", [P, 2, D], F32)
        scaled = sb("scaled", [P, NK, C], F32)
        mean_w = sb("mean_w", [P, P], F32)
        id32 = sb("id32", [P, P], F32)
        id16 = sb("id16", [P, P], BF16)
        ones = sb("ones", [P, NJ * H], F32)
        neg_d = sb("neg_d", [P, H, NK, 2], F32)
        big_d = sb("big_d", [P, H, NK, 2], F32)
        shifted = sb("shifted", [P, H, NJ], F32)
        above = sb("above", [P, 3, H, NJ], F32)
        edge = sb("edge", [P, 2, H, NJ], F32)
        edge_n = sb("edge_n", [P, 2, H, NJ], F32)
        alpha_next = sb("alpha_next", [P, 2, H, NJ], F32)
        alpha = sb("alpha", [P, 2, H, NJ], F32)
        fold_next = sb("fold_next", [P, H, C], F32)
        fold = sb("fold", [P, H, C], F32)
        small = sb("small", [P, 64], F32)
        top, top_all = small[:, 0:H + 1], small[:, 5:5 + H + 1]
        w_top = small[:, 10:14]
        recip, recip_w = small[:, 14:14 + NI], small[:, 22:22 + NI]
        stats = small[:, 30:42].rearrange("p (t n) -> p t n", t=2)
        moments = small[:, 42:46].rearrange("p (t n) -> p t n", t=2)
        var_eps, rstd, minus_half = small[:, 46:48], small[:, 48:50], small[:, 50:52]
        wh_sum = scaled.rearrange("p k c -> p (k c)")[:, 0:2 * H * F].rearrange("p (t h f) -> p t h f", t=2, h=H)
        top_quarters = small[:, 52:56]
        xT_first = pos.rearrange("p s k n -> p (s k n)").bitcast(F32)[:, 0:NJ * DC * P].rearrange(
            "p (q e c n) -> p q e c n", q=NK, e=2, c=DC)
        adj_first = neg.rearrange("p s k n -> p (s k n)").bitcast(I32).rearrange(
            "p (t i n) -> p t i n", t=4, i=2)
        tail_rows = wh.rearrange("p j h c -> p (j h c)")[:, 0:H * 2 * D].rearrange(
            "p (k e d) -> p k e d", k=H, e=2)
        sT = x_in[0:H * NK, 0, 0, :].rearrange("p (n e) -> p n e", e=2)
        a_bc = values[:, 0, :, :, :].rearrange("p a b c -> p (a b c)").bitcast(F32)[:, 0:2 * H * F]
        a_prod = values[:, 1, :, :, :].rearrange("p a b c -> p (a b c)").bitcast(F32)[:, 0:H * F]

        acc = pb("acc", [P, 4, 512], F32)
        adj_ps = pb("adj_ps", [P, NK, P], BF16)
        wh_ps = pb("wh_ps", [P, 2, 512], F32)
        x_ps = pb("x_ps", [P, 512], F32)
        xT_ps = x_ps[:, :].rearrange("p (e c n) -> p e c n", e=2, c=DC)
        sT_ps = wh_ps[0:H * NK, 0, 0:2 * P].rearrange("p (e n) -> p e n", e=2)

        waits_passed = sem("waits_passed")
        w_loaded = sem("w_loaded")
        x_loaded = [sem(f"x_loaded{i}") for i in range(2)]
        s_loaded = [sem(f"s_loaded{i}") for i in range(2)]
        resid_loaded = [sem(f"resid_loaded{i}") for i in range(2)]
        adj_loaded = [sem(f"adj_loaded{i}") for i in range(2)]
        adj_first_loaded = [sem(f"adj_first_loaded{i}") for i in range(8)]
        tail_loaded = sem("tail_loaded")
        s_stored = sem("s_stored")
        out_stored = [sem(f"out_stored{i}") for i in range(2)]
        consts_made = sem("consts_made")
        waug_made = sem("waug_made")
        adj_coded = sem("adj_coded")
        adj_turned = sem("adj_turned")
        adj_kept = sem("adj_kept")
        x_turned = sem("x_turned")
        x_kept = sem("x_kept")
        wh_made = sem("wh_made")
        wh_kept = sem("wh_kept")
        s_turned = sem("s_turned")
        s_kept = sem("s_kept")
        d_flipped = sem("d_flipped")
        big_made = sem("big_made")
        scalar_signs = sem("scalar_signs")
        vector_signs = sem("vector_signs")
        masks_made = sem("masks_made")
        sums_made = sem("sums_made")
        sums_kept = sem("sums_kept")
        sums_read = sem("sums_read")
        part_steps = sem("part_steps")
        recip_made = sem("recip_made")
        heads_made = sem("heads_made")
        values_scaled = sem("values_scaled")
        highs_made = sem("highs_made")
        values_made = sem("values_made")
        tops_made = sem("tops_made")
        tops_shared = sem("tops_shared")
        factor_steps = sem("factor_steps")
        exps_made = sem("exps_made")
        wh_added = sem("wh_added")
        mean_made = sem("mean_made")
        fold_made = sem("fold_made")
        latched = sem("latched")
        wtop_latched = sem("wtop_latched")
        elu_exp = sem("elu_exp")
        norm_steps = sem("norm_steps")
        rstd_made = sem("rstd_made")
        out_made = sem("out_made")

        NCONST = 9
        LEAD = 1
        VECTOR_FINISH = (0, 1)
        NT = 6
        NF = 9
        NS = 7
        NADD = NJ // 2 - 1
        TOPS_AT = [(4, 0), (4, 2), (5, 0), (5, 1)]
        ADDS_AT = {(4, 0): (0, 1), (4, 1): (2,), (4, 2): (3,), (4, 3): (4,), (5, 1): (5,), (5, 2): (6,)}

        def due(count):
            return not isinstance(count, int) or count > 0

        def apart(eng):
            eng.sem_inc(waits_passed, 1)

        def vector_comparisons(b, k, chunks=0):
            of_unit = [4 * NCH - sum(n) for n in ON_SCALAR]
            count = sum(of_unit) * b + sum(of_unit[0:k]) + sum(4 - n for n in ON_SCALAR[k][0:chunks])
            return count if k >= 0 else sum(of_unit) * b - of_unit[k]

        def batches(eng, body):
            body(0, True, False)
            with eng.Fori(1, B - 1) as b:
                body(b, False, False)
            body(B - 1, False, True)

        X_START = NI * 2 + 2

        def x_step(q):
            return 10 * q // 3

        def x_pairs_at(k, t, later):
            return [q for q in range(NK) if x_step(q) + later == NI * k + t - X_START]

        V_START = NCH * (UB - 2) + 2
        V_BEFORE = NCH * UB - V_START

        def value_step_at(b, k, c, last):
            if k < H:
                n = NCH * (UB + k) + c - V_START
                return None if n >= 4 * H else (b, n // 4, n % 4)
            n = NCH * k + c - V_START
            return None if last or n < 0 else (b + 1, n // 4, n % 4)

        X_LOADS = [(1, 1), (1, 3), (2, 1), (2, 2), (3, 0), (3, 2), (4, 0), (4, 1)]

        def before_loop(b):
            return isinstance(b, int) and b == 0

        def xT_of(b, q):
            return xT_first[:, q, :, :, :] if before_loop(b) else xT[:, :, :, :]

        def first_half(n):
            return isinstance(n, int) and n < NI

        def adj_in_of(n, i):
            return adj_first[:, n % 4, i, :] if first_half(n) else adj_in[:, i, :]

        def is_tail(b, k):
            return isinstance(b, int) and b == B - 1 and k >= H

        def rows_of(b, k):
            return tail_rows[:, k - H, :, :] if is_tail(b, k) else resid[:, k % 2, :, :]

        def finish_heads(eng, b, k):
            half, h = k // H, k % H
            u = UB * b + k
            eng.wait_ge(recip_made, 2 * (u + 1))
            if due(2 * (UB * b + half * H - H)):
                eng.wait_ge(out_made, 2 * (UB * b + half * H - H))
            eng.tensor_tensor(heads[:, half, :, h * F:(h + 1) * F], row[:, k % 2, :, 0:F],
                              recip_w[:, :].unsqueeze(2).to_broadcast([P, NI, F]), ALU.mult
                              ).then_inc(heads_made, 1)
            eng.wait_ge(heads_made, u + 1)

        block = ctx.enter_context(nc.Block())

        @block.sync
        def _(sp):
            def load_x(b, q):
                if due(NK * b + q - 1):
                    sp.wait_ge(x_turned, NK * b + q - 1)
                apart(sp)
                if q == 0:
                    if due(16 * b):
                        sp.wait_ge(s_stored, 16 * b)
                apart(sp)
                sp.dma_start(x_in[:, q % 2, :, :], x_pairs[b, q, :, :, :]).then_inc(x_loaded[q % 2], 16)

            def load_s(b, k):
                u = UB * b + k
                if k == 0:
                    sp.wait_ge(s_stored, 16 * (b + 1))
                    apart(sp)
                if due(NCH * (u - 1)):
                    sp.wait_ge(scalar_signs, NCH * (u - 1))
                apart(sp)
                if due(vector_comparisons(b, k - 1)):
                    sp.wait_ge(vector_signs, vector_comparisons(b, k - 1))
                apart(sp)
                half, h = k // H, k % H
                sp.dma_start(s_bc[:, k % 2, :],
                             s_rows[b, h:h + 1, half * HALF:(half + 1) * HALF].to_broadcast([P, HALF])
                             ).then_inc(s_loaded[k % 2], 16)

            def store_s(b):
                sp.wait_ge(s_kept, b + 1)
                apart(sp)
                sp.dma_start(s_rows[b, :, :].rearrange("h (k n) -> (h k) n", k=NK),
                             x_in[0:H * NK, 0, 0, :]).then_inc(s_stored, 16)

            def load_resid(b, k):
                if due(8 * (UB * b + k - k % 2)):
                    sp.wait_ge(out_stored[k % 2], 8 * (UB * b + k - k % 2))
                apart(sp)
                sp.dma_start(resid[:, k % 2, :, :], x_pairs[b, k, :, :, :]).then_inc(resid_loaded[k % 2], 16)

            def store_out(b, k):
                r = UB * b + k
                sp.wait_ge(out_made, 2 * (r + 1))
                apart(sp)
                sp.dma_start(out_pairs[b, k, :, :, :], rows_of(b, k)).then_inc(out_stored[k % 2], 16)

            for c in range(DC):
                sp.dma_start(w_aug[:, c, 0:D], w[c * P:(c + 1) * P, :]).then_inc(w_loaded, 16)
            for i, a in enumerate((a_src, a_dst)):
                sp.dma_start(a_bc[:, i * H * F:(i + 1) * H * F],
                             a.rearrange("(o h) f -> o (h f)", o=1).to_broadcast([P, H * F])
                             ).then_inc(w_loaded, 16)
            def load_adj(n, i):
                if due(2 * (n - (4 if first_half(n) else 1)) + i + 1):
                    sp.wait_ge(adj_coded, 2 * (n - (4 if first_half(n) else 1)) + i + 1)
                apart(sp)
                sp.dma_start(adj_in_of(n, i), adj_tiles[n, :, i * (N // 2):(i + 1) * (N // 2)]
                             ).then_inc(adj_first_loaded[2 * (n % 4) + i] if first_half(n)
                                        else adj_loaded[i], 16)

            for q in range(NK):
                load_x(0, q)
                if q % 2:
                    load_adj(q // 2, 0)
                    load_adj(q // 2, 1)
            for n in range(NI // 2, NI):
                load_adj(n, 0)
                load_adj(n, 1)
            store_s(0)
            load_s(0, 0)
            load_s(0, 1)
            for n in range(NI, NI + 4):
                load_adj(n, 0)
                load_adj(n, 1)
            load_adj(NI + 4, 0)

            def slot(b, k, first, last):
                if k < UB - 2:
                    load_s(b, k + 2)
                elif not last:
                    load_s(b + 1, k + 2 - UB)
                if not (first and k < 6):
                    store_out(b if k >= 6 else b - 1, (k - 6) % UB)
                if not (first and k < 4):
                    load_resid(b if k >= 4 else b - 1, (k - 4) % UB)
                for c in range(NCH):
                    n = 2 * k + NI + 4 + (c + 1) // 2
                    if not last or n < 2 * NI:
                        load_adj(2 * NI * b + n, (c + 1) % 2)
                    if not last and (k, c) in X_LOADS:
                        load_x(b + 1, X_LOADS.index((k, c)))
                if k == UB - 3 and not last:
                    store_s(b + 1)
                if k == H and last:
                    sp.wait_ge(values_made, 4 * H * B)
                    for n in range(H):
                        sp.dma_start(tail_rows[:, n, :, :], x_pairs[b, H + n, :, :, :]).then_inc(tail_loaded, 16)

            def body(b, first, last):
                for k in range(UB):
                    slot(b, k, first, last)

            batches(sp, body)
            for k in range(2, UB):
                store_out(B - 1, k)
            for i in range(2):
                sp.wait_ge(out_stored[i], 16 * UB * B // 2)

        @block.gpsimd
        def _(pool):
            def scale_values(b, h, i):
                g, t0 = i // 2, (i % 2) * NK
                step = 4 * (H * b + h) + i
                if i == 0:
                    pool.wait_ge(factor_steps, NF * (b + 1))
                if i == 0 and h == 0:
                    pool.wait_ge(mean_made, b + 1)
                if due(step):
                    pool.wait_ge(values_made, step)
                pool.tensor_tensor(scaled[:, :, :], wh[:, t0:t0 + NK, h, :],
                                   edge_n[:, g, h, t0:t0 + NK].unsqueeze(2).to_broadcast([P, NK, C]),
                                   ALU.mult).then_inc(values_scaled, 1)

            def low_values(b, h, i):
                g, t0 = i // 2, (i % 2) * NK
                step = 4 * (H * b + h) + i
                pool.wait_ge(highs_made, step + 1)
                pool.tensor_tensor(values[:, h, t0:t0 + NK, g, C:2 * C], scaled[:, :, :],
                                   values[:, h, t0:t0 + NK, g, 0:C], ALU.subtract).then_inc(values_made, 1)

            def share_tops(b):
                pool.wait_ge(tops_made, NT * (b + 1))
                apart(pool)
                pool.partition_all_reduce(top_all[:, :], top[:, :], P, bass.bass_isa.ReduceOp.max
                                          ).then_inc(tops_shared, 1)

            def add_wh(b, adds):
                for i in adds:
                    a = wh[:, 0:2, :, 0:F] if i == 0 else wh_sum[:, :, :, :]
                    pool.wait_ge(wh_kept, 2 * (NK * b + i + 2))
                    if i == 0:
                        if due(4 * H * b):
                            pool.wait_ge(values_made, 4 * H * b)
                    if due(NADD * b + i):
                        pool.wait_ge(wh_added, NADD * b + i)
                    pool.tensor_tensor(wh_sum[:, :, :, :], a, wh[:, 2 * i + 2:2 * i + 4, :, 0:F],
                                       ALU.add).then_inc(wh_added, 1)

            def latch(b):
                pool.wait_ge(exps_made, 4 * (b + 1))
                pool.wait_ge(fold_made, b + 1)
                if due(3 * NP * UB * b):
                    pool.wait_ge(part_steps, 3 * NP * UB * b)
                apart(pool)
                pool.tensor_scalar(alpha[:, :, :, :], alpha_next[:, :, :, :], 1.0, 0.0, ALU.mult, ALU.add
                                   ).then_inc(latched, 1)
                pool.tensor_scalar(fold[:, :, :], fold_next[:, :, :], 1.0, 0.0, ALU.mult, ALU.add
                                   ).then_inc(latched, 1)
                pool.wait_ge(latched, 2 * (b + 1))

            def epilogue(b, k, c):
                half, h, i = k // H, k % H, c % 2
                m = NP * (UB * b + k) + c
                t0 = half * NI + 2 * c
                s = sums[:, i, :, :, :]
                pool.wait_ge(sums_kept, m + 1)
                if c == 0:
                    if due(UB * b + k - 1):
                        pool.wait_ge(heads_made, UB * b + k - 1)
                if due(3 * m):
                    pool.wait_ge(part_steps, 3 * m)
                pool.tensor_tensor(part[:, :, :, :], s[:, :, :, 0:C], s[:, :, :, C:2 * C], ALU.add
                                   ).then_inc(sums_read, 1)
                pool.wait_ge(sums_read, m + 1)
                al = alpha[:, :, h, t0:t0 + 2].rearrange("p g t -> p t g").unsqueeze(3)
                pool.tensor_tensor(part[:, :, :, :], part[:, :, :, :], al.to_broadcast([P, 2, 2, C]),
                                   ALU.mult).then_inc(part_steps, 1)
                pool.wait_ge(part_steps, 3 * m + 1)
                r = row[:, k % 2, 2 * c:2 * c + 2, :]
                pool.tensor_tensor(r, part[:, :, 0, :], part[:, :, 1, :], ALU.add).then_inc(part_steps, 1)
                pool.wait_ge(part_steps, 3 * m + 2)
                pool.tensor_tensor(r, r, fold[:, h, :].unsqueeze(1).to_broadcast([P, 2, C]), ALU.add
                                   ).then_inc(part_steps, 1)

            def inv_std(b, k):
                r = UB * b + k
                pool.wait_ge(norm_steps, NS * (r + 1))
                pool.tensor_tensor(rstd[:, :], var_eps[:, :], minus_half[:, :], ALU.pow).then_inc(rstd_made, 1)

            for ident in (id32, id16):
                pool.memset(ident[:, :], 0.0).then_inc(consts_made, 1)
            pool.memset(mean_w[:, :], TINY / N).then_inc(consts_made, 1)
            pool.memset(minus_half[:, :], -0.5).then_inc(consts_made, 1)
            pool.memset(ones[:, :], 1.0).then_inc(consts_made, 1)
            pool.memset(fold_next[:, :, :], TINY).then_inc(consts_made, 1)
            pool.memset(wh[:, :, :, F:C], 1.0).then_inc(consts_made, 1)
            pool.wait_ge(consts_made, NCONST - 2)
            for ident in (id32, id16):
                pool.affine_select(out=ident[:, :], in_=ident[:, :], compare_op=ALU.not_equal, fill=1.0, base=0,
                                   pattern=[[-1, P]], channel_multiplier=1).then_inc(consts_made, 1)
            add_wh(0, range(NADD))
            share_tops(0)
            for n in range(V_BEFORE):
                scale_values(0, n // 4, n % 4)
                low_values(0, n // 4, n % 4)

            def slot(b, k, first, last):
                if k == 0:
                    latch(b)
                for c in range(NP):
                    v = value_step_at(b, k, c, last)
                    if v:
                        scale_values(*v)
                    if k == UB - 3 and c == 3 and not last:
                        share_tops(b + 1)
                    if c == 3 and not (first and k < 5):
                        inv_std(b if k >= 5 else b - 1, (k - 5) % UB)
                    epilogue(b, k, c)
                    if v:
                        low_values(*v)
                    if c == 1 and not (first and k == 0) and k not in VECTOR_FINISH:
                        finish_heads(pool, b if k else b - 1, (k - 1) % UB)
                    if not last:
                        add_wh(b + 1, ADDS_AT.get((k, c), ()))

            def body(b, first, last):
                for k in range(UB):
                    slot(b, k, first, last)

            batches(pool, body)
            inv_std(B - 1, 3)
            finish_heads(pool, B - 1, UB - 1)
            for k in range(4, UB):
                inv_std(B - 1, k)

        @block.scalar
        def _(act):
            def keep_xT(b, q):
                act.wait_ge(x_turned, NK * b + q + 1)
                if not before_loop(b):
                    act.wait_ge(wh_made, NK * b + q)
                act.activation(xT_of(b, q), xT_ps, ACT.Copy).then_inc(x_kept, 1)

            def keep_wh(b, q):
                act.wait_ge(wh_made, NK * b + q + 1)
                if q == 0:
                    if due(4 * H * b):
                        act.wait_ge(values_made, 4 * H * b)
                    if due(NADD * b):
                        act.wait_ge(wh_added, NADD * b)
                    if due(NF * b):
                        act.wait_ge(factor_steps, NF * b)
                    if due(b):
                        act.wait_ge(d_flipped, b)
                    if due(b):
                        act.wait_ge(s_turned, b)
                act.activation(wh[:, 2 * q:2 * q + 2, :, 0:F],
                               wh_ps[:, :, 0:D].rearrange("p e (h f) -> p e h f", h=H), ACT.Copy
                               ).then_inc(wh_kept, 1)
                act.activation(sd[:, :, q, :], wh_ps[:, :, D:WC].rearrange("p e c -> p c e"), ACT.Copy
                               ).then_inc(wh_kept, 1)

            def factor_exps(b):
                def f(n):
                    act.wait_ge(factor_steps, NF * b + n)
                if due(2 * b):
                    act.wait_ge(latched, 2 * b)
                f(4)
                act.activation(edge[:, 0, :, :], shifted[:, :, :], ACT.Exp).then_inc(exps_made, 1)
                act.activation(edge[:, 1, :, :], shifted[:, :, :], ACT.Exp, scale=SLOPE).then_inc(exps_made, 1)
                f(7)
                act.activation(alpha_next[:, 0, :, :], above[:, 1, :, :], ACT.Exp, scale=1 - SLOPE
                               ).then_inc(exps_made, 1)
                act.activation(alpha_next[:, 1, :, :], above[:, 2, :, :], ACT.Exp, scale=SLOPE - 1
                               ).then_inc(exps_made, 1)

            def make_big(b):
                act.wait_ge(wh_kept, 2 * NK * (b + 1))
                if due(NCH * UB * b):
                    act.wait_ge(scalar_signs, NCH * UB * b)
                act.activation(big_d[:, :, :, :], sd[:, H:2 * H, :, :], ACT.Copy, scale=BIG).then_inc(big_made, 1)
                act.wait_ge(big_made, b + 1)

            def signs(b, k, c, values=None):
                h = k % H
                m = NCH * (UB * b + k) + c
                if c == 0:
                    act.wait_ge(s_loaded[k % 2], 8 * (UB * b + k - k % 2) + 16)
                if due(2 * (m - 1)):
                    act.wait_ge(masks_made, 2 * (m - 1))
                apart(act)
                for i in range(ON_SCALAR[k][c]):
                    kk, e = i // 2, i % 2
                    if i == 2 and values:
                        high_values(*values)
                    a = act.activation(sign[:, c % 2, kk, e:2 * HALF:2].bitcast(F8), s_bc[:, k % 2, :], ACT.Relu,
                                       bias=big_d[:, h, 2 * c + kk, e:e + 1], scale=BIG, saturate=False)
                a.then_inc(scalar_signs, 1)

            def keep_sums(b, k, c):
                m = NP * (UB * b + k) + c
                bank = (2 * c) % 4
                act.wait_ge(sums_made, m + 1)
                if due(m - 1):
                    act.wait_ge(sums_read, m - 1)
                act.activation(sums[:, c % 2, :, :, :].rearrange("p t g n -> p t (g n)"),
                               acc[:, bank:bank + 2, 0:4 * C], ACT.Copy).then_inc(sums_kept, 1)

            def elu_part(b, k):
                half, c, r = k // H, k % H, UB * b + k
                act.wait_ge(heads_made, UB * b + (half + 1) * H)
                if due(NS * (r - 1) + 2):
                    act.wait_ge(norm_steps, NS * (r - 1) + 2)
                act.activation(expo[:, :, :], heads[:, half, 2 * c:2 * c + 2, :], ACT.Exp).then_inc(elu_exp, 1)

            def high_values(b, h, i):
                g, t0 = i // 2, (i % 2) * NK
                step = 4 * (H * b + h) + i
                act.wait_ge(values_scaled, step + 1)
                if i == 0:
                    if due(NP * (UB * b - H + h + 1)):
                        act.wait_ge(sums_made, NP * (UB * b - H + h + 1))
                act.activation(values[:, h, t0:t0 + NK, g, 0:C], scaled[:, :, :], ACT.Copy).then_inc(highs_made, 1)

            keep_xT(0, 0)
            for q in range(NK):
                if q + 1 < NK:
                    keep_xT(0, q + 1)
                keep_wh(0, q)
            make_big(0)
            factor_exps(0)
            for c in range(NCH):
                before, amid = ((0, 1), (None, 2), (3, 4), (None, 5))[c]
                if before is not None:
                    high_values(0, before // 4, before % 4)
                signs(0, 0, c, (0, amid // 4, amid % 4))
            for c in range(LEAD):
                signs(0, 1, c)

            def slot(b, k, first, last):
                for c in range(NCH):
                    if not last:
                        for t in (2 * c, 2 * c + 1):
                            for q in x_pairs_at(k, t, 4):
                                keep_wh(b + 1, q)
                            for q in x_pairs_at(k, t, 1):
                                keep_xT(b + 1, q)
                    ahead = k + 1 + (c + LEAD) // NCH
                    if ahead == UB and c + LEAD == NCH and not last:
                        make_big(b + 1)
                    v = value_step_at(b, k if c else k - 1, (c - 1) % NCH, last)
                    if first and k == 0 and c == 0:
                        v = None
                    if ahead < UB:
                        signs(b, ahead, (c + LEAD) % NCH, v)
                    elif not last:
                        signs(b + 1, ahead - UB, (c + LEAD) % NCH, v)
                    if c == 3 and not (first and k < 4):
                        elu_part(b if k >= 4 else b - 1, (k - 4) % UB)
                    keep_sums(b, k, c)
                    if c == 0 and k == UB - 2 and not last:
                        factor_exps(b + 1)

            def body(b, first, last):
                for k in range(UB):
                    slot(b, k, first, last)

            batches(act, body)
            for k in range(4, UB):
                elu_part(B - 1, k)

        @block.vector
        def _(dve):
            def code_adj(n, i, half):
                if first_half(n):
                    dve.wait_ge(adj_first_loaded[2 * (n % 4) + half], 16 * (n // 4 + 1))
                else:
                    dve.wait_ge(adj_loaded[half], 16 * (n - NI + 1))
                if half == 0:
                    if due(n - 1):
                        dve.wait_ge(adj_turned, n - 1)
                dve.tensor_scalar(adj_code[:, i, half * (N // 2):(half + 1) * (N // 2)], adj_in_of(n, half),
                                  0.0, float(ONE - 1), ALU.is_gt, ALU.add).then_inc(adj_coded, 1)

            def keep_adj(n, g, half, t):
                dve.wait_ge(adj_turned, n + 1)
                if due(2 * NCH * H * (g - 1)):
                    dve.wait_ge(masks_made, 2 * NCH * H * (g - 1))
                dve.tensor_copy(adjT[:, half, :, 2 * t * P:2 * (t + 1) * P].bitcast(I32),
                                adj_ps[:, :, :].bitcast(I32)).then_inc(adj_kept, 1)

            def keep_s(b):
                dve.wait_ge(s_turned, b + 1)
                dve.wait_ge(x_turned, NK * (b + 1))
                dve.tensor_copy(sT.rearrange("p n e -> p e n"), sT_ps).then_inc(s_kept, 1)

            def tops(b, i):
                n = NJ // 4
                done = NT * b + i
                dve.wait_ge(wh_kept, 2 * (NK * b + (i + 1) * n // 2))
                if i == 0:
                    if due(b):
                        dve.wait_ge(tops_shared, b)
                dve.tensor_reduce(top_quarters[:, i:i + 1], wh[:, i * n:(i + 1) * n, :, 0:F], AX.XYZ, ALU.max,
                                  apply_absolute_value=True).then_inc(tops_made, 1)
                if i == 3:
                    dve.tensor_reduce(top[:, 0:H], sd[:, H:2 * H, :, :], AX.XY, ALU.max).then_inc(tops_made, 1)
                    dve.wait_ge(tops_made, done + 2)
                    dve.tensor_reduce(top[:, H:H + 1], top_quarters, AX.X, ALU.max).then_inc(tops_made, 1)

            def factors(b):
                n = [0]

                def step(ins):
                    n[0] += 1
                    ins.then_inc(factor_steps, 1)
                    dve.wait_ge(factor_steps, NF * b + n[0])

                s = sd[:, 0:H, :, :].rearrange("p h k e -> p h (k e)")
                d = sd[:, H:2 * H, :, :].rearrange("p h k e -> p h (k e)")
                D_bc = top_all[:, 0:H].unsqueeze(2).to_broadcast([P, H, NJ])
                dve.wait_ge(tops_shared, b + 1)
                if due(b):
                    dve.wait_ge(wtop_latched, b)
                step(dve.tensor_scalar(w_top[:, 0:1], top_all[:, H:H + 1], 1e-30, None, ALU.max))
                step(dve.reciprocal(w_top[:, 1:2], w_top[:, 0:1]))
                step(dve.tensor_scalar(w_top[:, 2:3], w_top[:, 1:2], VSCALE, None, ALU.mult))
                step(dve.tensor_tensor(shifted[:, :, :], d, D_bc, ALU.subtract))
                step(dve.tensor_tensor(above[:, 0, :, :], s, D_bc, ALU.add))
                step(dve.tensor_scalar(above[:, 1, :, :], above[:, 0, :, :], 0.0, None, ALU.min))
                step(dve.tensor_scalar(above[:, 2, :, :], above[:, 0, :, :], 0.0, None, ALU.max))

            def factors_end(b):
                dve.tensor_scalar(wh[:, :, :, F], ones[:, :].rearrange("p (j h) -> p j h", h=H), w_top[:, 0:1], None,
                                  ALU.mult).then_inc(factor_steps, 1)
                dve.wait_ge(exps_made, 4 * b + 2)
                if due(4 * H * b):
                    dve.wait_ge(values_made, 4 * H * b)
                dve.tensor_scalar(edge_n[:, :, :, :], edge[:, :, :, :], w_top[:, 2:3], None, ALU.mult
                                  ).then_inc(factor_steps, 1)

            def make_fold(b):
                dve.wait_ge(mean_made, b + 1)
                if due(2 * b):
                    dve.wait_ge(latched, 2 * b)
                dve.tensor_scalar(fold_next[:, :, 0:F], wh_ps[:, 1, 0:H * F].rearrange("p (h f) -> p h f", h=H),
                                  w_top[:, 1:2], None, ALU.mult).then_inc(fold_made, 1)

            def flip_d(b):
                if due(vector_comparisons(b, 0)):
                    dve.wait_ge(vector_signs, vector_comparisons(b, 0))
                dve.tensor_scalar(neg_d[:, :, :, :], sd[:, H:2 * H, :, :], -1.0, None, ALU.mult
                                  ).then_inc(d_flipped, 1)
                dve.wait_ge(d_flipped, b + 1)

            def signs(b, k, c):
                h = k % H
                m = NCH * (UB * b + k) + c
                if c == 0:
                    dve.wait_ge(s_loaded[k % 2], 8 * (UB * b + k - k % 2) + 16)
                for i in range(ON_SCALAR[k][c], 4):
                    kk, e = i // 2, i % 2
                    if due(2 * (m - 1)):
                        dve.wait_ge(masks_made, 2 * (m - 1))
                    dve.tensor_scalar(sign[:, c % 2, kk, e:2 * HALF:2], s_bc[:, k % 2, :],
                                      neg_d[:, h, 2 * c + kk, e:e + 1], float(ONE), ALU.is_gt, ALU.mult
                                      ).then_inc(vector_signs, 1)

            def masks(b, k, c):
                half, u = k // H, UB * b + k
                m = NCH * u + c
                if c == 0:
                    dve.wait_ge(adj_kept, NI * (2 * b + half + 1))
                    if due(NP * (u - 1)):
                        dve.wait_ge(sums_made, NP * (u - 1))
                dve.wait_ge(scalar_signs, m + 1)
                dve.wait_ge(vector_signs, vector_comparisons(b, k, c + 1))

                def words(t):
                    return t.rearrange("p k n -> p (k n)").bitcast(I32)
                sg = words(sign[:, c % 2, :, :])
                ad = words(adjT[:, half, 2 * c:2 * c + 2, :])
                dve.tensor_tensor(words(pos[:, k % 2, 2 * c:2 * c + 2, :]), sg, ad, ALU.bitwise_and
                                  ).then_inc(masks_made, 1)
                dve.scalar_tensor_tensor(words(neg[:, k % 2, 2 * c:2 * c + 2, :]), sg, ONES, ad,
                                         ALU.bitwise_xor, ALU.bitwise_and).then_inc(masks_made, 1)

            def make_recip(b, k, i):
                u = UB * b + k
                if i == 0:
                    dve.wait_ge(part_steps, 3 * NP * (u + 1))
                    if due(u):
                        dve.wait_ge(heads_made, u)
                    dve.reciprocal(recip[:, :], row[:, k % 2, :, F]).then_inc(recip_made, 1)
                else:
                    dve.wait_ge(recip_made, 2 * u + 1)
                    dve.tensor_scalar(recip_w[:, :], recip[:, :], w_top[:, 3:4], None, ALU.mult
                                      ).then_inc(recip_made, 1)

            def latch_top(b):
                dve.wait_ge(factor_steps, NF * b + 1)
                if due(2 * UB * b):
                    dve.wait_ge(recip_made, 2 * UB * b)
                dve.tensor_copy(w_top[:, 3:4], w_top[:, 0:1]).then_inc(wtop_latched, 1)
                dve.wait_ge(wtop_latched, b + 1)

            def norm_start(b, k, part):
                half, c, i, r = k // H, k % H, k % 2, UB * b + k
                res = rows_of(b, k)
                if part == 0:
                    dve.wait_ge(elu_exp, r + 1)
                    if is_tail(b, k):
                        dve.wait_ge(tail_loaded, 16 * H)
                    else:
                        dve.wait_ge(resid_loaded[i], 8 * (UB * b + k - i) + 16)
                    dve.scalar_tensor_tensor(expo[:, :, :], expo[:, :, :], 1.0, res, ALU.min, ALU.add
                                             ).then_inc(norm_steps, 1)
                elif part == 1:
                    dve.wait_ge(norm_steps, NS * r + 1)
                    dve.scalar_tensor_tensor(res, heads[:, half, 2 * c:2 * c + 2, :], 0.0, expo[:, :, :],
                                             ALU.max, ALU.add).then_inc(norm_steps, 1)
                elif part == 2:
                    dve.wait_ge(norm_steps, NS * r + 2)
                    for t in range(2):
                        dve.bn_stats(stats[:, t, :], res[:, t, :]).then_inc(norm_steps, 1)
                elif part == 3:
                    dve.wait_ge(norm_steps, NS * r + 4)
                    apart(dve)
                    for t in range(2):
                        dve.bn_aggr(moments[:, t, :], stats[:, t, :]).then_inc(norm_steps, 1)
                else:
                    dve.wait_ge(norm_steps, NS * r + 6)
                    if due(r):
                        dve.wait_ge(rstd_made, r)
                    dve.tensor_scalar(var_eps[:, :], moments[:, :, 1], 1e-5, None, ALU.add
                                      ).then_inc(norm_steps, 1)

            def norm_end(b, k):
                r, res = UB * b + k, rows_of(b, k)
                dve.wait_ge(rstd_made, r + 1)
                for t in range(2):
                    dve.tensor_scalar(res[:, t, :], res[:, t, :], moments[:, t, 0:1], rstd[:, t:t + 1],
                                      ALU.subtract, ALU.mult).then_inc(out_made, 1)
                dve.wait_ge(out_made, 2 * (r + 1))

            dve.wait_ge(w_loaded, 16 * (DC + 2))
            done = 0
            for c in range(DC):
                for i in range(2):
                    if due(done):
                        dve.wait_ge(waug_made, done)
                    dve.tensor_tensor(a_prod, w_aug[:, c, 0:D], a_bc[:, i * D:(i + 1) * D], ALU.mult
                                      ).then_inc(waug_made, 1)
                    dve.wait_ge(waug_made, done + 1)
                    dve.tensor_reduce(w_aug[:, c, D + i * H:D + (i + 1) * H],
                                      a_prod.rearrange("p (h f) -> p h f", h=H), AX.X, ALU.add
                                      ).then_inc(waug_made, 1)
                    done += 2
            for n in range(NI):
                code_adj(n, n % 2, 0)
                code_adj(n, n % 2, 1)
                if n:
                    keep_adj(n - 1, 0, 0, n - 1)
                if n < 4:
                    tops(0, n)
                if n == 3:
                    keep_s(0)
                    flip_d(0)
                    factors(0)
                if n == 4:
                    factors_end(0)
                    make_fold(0)
            keep_adj(NI - 1, 0, 0, NI - 1)
            signs(0, 0, 0)
            for c in range(NCH):
                n = NI + c
                if c >= 2:
                    keep_adj(n - 2, 1, 1, c - 2)
                code_adj(n, n % 2, 0)
                if c < NCH - 1:
                    code_adj(n, n % 2, 1)
                masks(0, 0, c)
                signs(0, (c + 1) // NCH, (c + 1) % NCH)

            def slot(b, k, first, last):
                more = not (last and k == UB - 1)
                nb, nk = (b, k + 1) if k < UB - 1 else (b + 1, 0)
                turn = not last or k < H - 1
                code = not last or k < H - 2
                n0 = 2 * NI * b + 2 * k + NI + 2
                g = 2 * nb + nk // H + 1
                half, t0 = (nk // H + 1) % 2, 2 * (nk % H)
                for c in range(NCH):
                    if more:
                        masks(nb, nk, c)
                        if c < NCH - 1:
                            signs(nb, nk, c + 1)
                        elif k < UB - 2:
                            signs(b, k + 2, 0)
                        elif k == UB - 2 and not last:
                            flip_d(b + 1)
                            signs(b + 1, 0, 0)
                        elif k == UB - 1:
                            signs(b + 1, 1, 0)
                    recips = c == 1 and not (first and k == 0)
                    before = (b if k else b - 1, (k - 1) % UB)
                    norms = c in (1, 2) and not (first and k < 5)
                    piece = (b if k >= 5 else b - 1, (k - 5) % UB)
                    if recips:
                        make_recip(*before, 0)
                    if norms:
                        norm_start(*piece, 0 if c == 1 else 3)
                    if recips:
                        make_recip(*before, 1)
                    if c == 1 and turn:
                        keep_adj(n0, g, half, t0)
                    if c == 1 and k == 0:
                        latch_top(b)
                    if norms and c == 1:
                        norm_start(*piece, 1)
                    if recips and k in VECTOR_FINISH:
                        finish_heads(dve, *before)
                    if c == 3 and turn:
                        keep_adj(n0 + 1, g, half, t0 + 1)
                    if c == 0 and turn:
                        code_adj(n0 + 1, 1, 1)
                    elif c and code:
                        code_adj(n0 + 2 + c // 3, c // 3, int(c == 2))
                    if norms:
                        norm_start(*piece, 2 if c == 1 else 4)
                    if c == 0 and not (first and k < 6):
                        norm_end(b if k >= 6 else b - 1, (k - 6) % UB)
                    if k == UB - 3 and c == 2 and not last:
                        keep_s(b + 1)
                    if (k, c) in TOPS_AT and not last:
                        tops(b + 1, TOPS_AT.index((k, c)))
                    if k == UB - 2 and not last:
                        if c == 0:
                            factors(b + 1)
                        if c == 1:
                            factors_end(b + 1)
                        if c == 2:
                            make_fold(b + 1)

            def body(b, first, last):
                for k in range(UB):
                    slot(b, k, first, last)

            batches(dve, body)
            norm_end(B - 1, 2)
            for part in range(5):
                norm_start(B - 1, 3, part)
            norm_end(B - 1, 3)
            for i in range(2):
                make_recip(B - 1, UB - 1, i)
            for k in range(4, UB):
                for part in range(3):
                    norm_start(B - 1, k, part)
                if k > 4:
                    norm_end(B - 1, k - 1)
                for part in (3, 4):
                    norm_start(B - 1, k, part)
            norm_end(B - 1, UB - 1)

        @block.tensor
        def _(pe):
            def turn_adj(n, i):
                pe.wait_ge(adj_coded, 2 * (n + 1))
                if due(n):
                    pe.wait_ge(adj_kept, n)
                for kk in range(NK):
                    t = pe.transpose(adj_ps[:, kk, :],
                                     adj_code[:, i, 2 * P * kk:2 * P * (kk + 1)].bitcast(BF16), id16[:, :])
                t.then_inc(adj_turned, 1)

            def turn_x(b, q):
                pe.wait_ge(x_loaded[q % 2], 16 * (NK // 2 * b + q // 2 + 1))
                if due(NK * b + q):
                    pe.wait_ge(x_kept, NK * b + q)
                for e in range(2):
                    for c in range(DC):
                        t = pe.transpose(xT_ps[:, e, c, :], x_in[:, q % 2, e, c * P:(c + 1) * P], id32[:, :])
                t.then_inc(x_turned, 1)

            def project(b, q):
                pe.wait_ge(x_kept, NK * b + q + 1)
                if due(2 * (NK * b + q)):
                    pe.wait_ge(wh_kept, 2 * (NK * b + q))
                if q == 0:
                    if due(b):
                        pe.wait_ge(fold_made, b)
                for e in range(2):
                    for c in range(DC):
                        t = pe.matmul(wh_ps[:, e, 0:WC], xT_of(b, q)[:, e, c, :], w_aug[:, c, :],
                                      start=(c == 0), stop=(c == DC - 1))
                t.then_inc(wh_made, 1)

            def turn_s(b):
                pe.wait_ge(wh_kept, 2 * NK * (b + 1))
                for e in range(2):
                    t = pe.transpose(sT_ps[:, e, :], sd[:, 0:H, :, e].rearrange("p h k -> p (h k)"), id32[:, :])
                t.then_inc(s_turned, 1)

            def mean(b):
                pe.wait_ge(wh_added, NADD * (b + 1))
                for t in range(2):
                    m = pe.matmul(wh_ps[:, 1, 0:H * F], mean_w[:, :], wh_sum[:, t, :, :].rearrange("p h f -> p (h f)"),
                                  start=(t == 0), stop=(t == 1))
                m.then_inc(mean_made, 1)

            def row_tile(b, k, t):
                h = k % H
                m = NP * (UB * b + k) + t // 2
                if t == 0:
                    pe.wait_ge(masks_made, 2 * NCH * (UB * b + k + 1))
                    pe.wait_ge(values_made, 4 * (H * b + h + 1))
                if t % 2 == 0:
                    if due(m - 1):
                        pe.wait_ge(sums_kept, m - 1)
                    apart(pe)
                for g, mask in enumerate((pos, neg)):
                    rows = mask[:, k % 2, :, :].rearrange("p k (q n r e) -> p k q r e n", n=P, r=2, e=2)
                    for j in range(NJ):
                        i = pe.matmul(acc[:, t % 4, 2 * C * g:2 * C * (g + 1)],
                                      rows[:, j // 2, t // 2, t % 2, j % 2, :].bitcast(F8),
                                      values[:, h, j, g, :], start=(j == 0), stop=(j == NJ - 1))
                if t % 2:
                    i.then_inc(sums_made, 1)

            pe.wait_ge(consts_made, NCONST)
            turn_x(0, 0)
            pe.wait_ge(waug_made, 4 * DC)
            for q in range(NK):
                if q + 1 < NK:
                    turn_x(0, q + 1)
                project(0, q)
                if q % 2:
                    turn_adj(q // 2, q // 2 % 2)
            turn_s(0)
            mean(0)
            for n in range(NK // 2, NI + 2):
                turn_adj(n, n % 2)

            def slot(b, k, first, last):
                for t in range(NI):
                    if not last:
                        for q in x_pairs_at(k, t, 3):
                            project(b + 1, q)
                        for q in x_pairs_at(k, t, 0):
                            turn_x(b + 1, q)
                    if t == 5 and k == UB - 3 and not last:
                        turn_s(b + 1)
                    if t == 1 and k == UB - 2 and not last:
                        mean(b + 1)
                    row_tile(b, k, t)
                    if t in (2, 5) and (not last or k < H - 1):
                        n = 2 * NI * b + 2 * k + NI + 2 + (t == 5)
                        turn_adj(n, int(t == 5))

            def body(b, first, last):
                for k in range(UB):
                    slot(b, k, first, last)

            batches(pe, body)


_INS = ['x', 'adj', 'L0_gnn_W', 'L0_gnn_a_src', 'L0_gnn_a_dst']


def kernel(**inputs):
    import numpy as _np
    import concourse.bacc as _bacc
    from concourse import mybir as _mybir
    from concourse.bass_utils import run_bass_kernel_spmd as _run

    nc = _bacc.Bacc("TRN2", target_bir_lowering=False, num_devices=1, dynamic_dma_scratch_size=2048)
    arrays, args = {}, []
    for name in _INS:
        a = _np.ascontiguousarray(inputs[name])
        arrays[f"in_{name}_dram"] = a
        args.append(nc.dram_tensor(f"in_{name}_dram", a.shape, _mybir.dt.from_np(a.dtype), kind="ExternalInput").ap())
    shape = inputs['x'].shape
    args.append(nc.dram_tensor("out_0_dram", shape, _mybir.dt.float32, kind="ExternalOutput").ap())
    gat_resnorm(nc, *args)
    r = _run(nc, [arrays], core_ids=[0])
    return r.results[0]["out_0_dram"]
```
